# Optimizing a Trainium2 kernel written in Bass

```python
import numpy as np
import jax
import jax.numpy as jnp

def _softmax(x, axis=-1):
    return jax.nn.softmax(x, axis=axis)

def _gelu(x):
    return jax.nn.gelu(x, approximate=True)

def _silu(x):
    return jax.nn.silu(x)

def _sigmoid(x):
    return jax.nn.sigmoid(x)

def _layernorm(x, axis=-1, eps=1e-05):
    m = jnp.mean(x, axis=axis, keepdims=True)
    v = jnp.var(x, axis=axis, keepdims=True)
    return (x - m) / jnp.sqrt(v + eps)

def _scatter_add(tgt, idx, src, axis=0):
    return tgt.at[idx].add(src)

def _segment_sum(src, seg, n):
    return jax.ops.segment_sum(src, seg, n)
kernel_name = 'mk_adaln_d1_jaxref_r4_85f897'

def setup_inputs(seed: int=0):
    np.random.seed(seed)
    _w = jnp.asarray

    def _L0_attn_setup():
        import jax, jax.numpy as jnp
        import numpy as np
        import math
        B, T, D_IN, D_OUT = (2, 512, 1024, 1024)
        N_HEADS, N_KV = (32, 8)
        HEAD_DIM = D_OUT // N_HEADS
        GROUP_SIZE = N_HEADS // N_KV
        ROPE_BASE = 500000.0
        CTX = 512

        def _rope_tables(head_dim, base, seq_len):
            inv_freq = 1.0 / base ** (jnp.arange(0, head_dim, 2, dtype=jnp.float32) / head_dim)
            t = jnp.arange(seq_len, dtype=jnp.float32)
            freqs = jnp.einsum('i,j->ij', t, inv_freq)
            return (jnp.cos(freqs), jnp.sin(freqs))

        def _apply_rope(x, cos, sin):
            x1, x2 = jnp.split(x, 2, axis=-1)
            c = cos[None, None]
            s = sin[None, None]
            return jnp.concatenate([x1 * c - x2 * s, x1 * s + x2 * c], axis=-1)
        key = jax.random.key(seed)
        ks = jax.random.split(key, 5)
        scale = 0.02
        return {'x': jax.random.normal(ks[0], (B, T, D_IN), dtype=jnp.float32), 'Wq': jax.random.normal(ks[1], (D_IN, D_OUT), dtype=jnp.float32) * scale, 'Wk': jax.random.normal(ks[2], (D_IN, N_KV * HEAD_DIM), dtype=jnp.float32) * scale, 'Wv': jax.random.normal(ks[3], (D_IN, N_KV * HEAD_DIM), dtype=jnp.float32) * scale, 'Wo': jax.random.normal(ks[4], (D_OUT, D_OUT), dtype=jnp.float32) * scale}
    _L0_attn_in = _L0_attn_setup()

    def _L0_ffn_setup():
        import jax, jax.numpy as jnp
        import numpy as np
        R = 16
        LORA_ALPHA = 16
        SCALING = LORA_ALPHA / R
        key = jax.random.key(seed)
        kx, kr, ka = jax.random.split(key, 3)
        B, S, D, DO, E = (4, 512, 1024, 1024, 8)
        x = jax.random.normal(kx, (B, S, D), dtype=jnp.float32)
        bound_r = 1.0 / np.sqrt(D)
        route_w = jax.random.uniform(kr, (E, D), jnp.float32, -bound_r, bound_r)
        bound_a = 1.0 / np.sqrt(D)
        A = jax.random.uniform(ka, (E, R, D), jnp.float32, -bound_a, bound_a)
        kb = jax.random.fold_in(key, 7)
        Bw = jax.random.normal(kb, (E, DO, R), dtype=jnp.float32) * 0.02
        return {'x': x, 'route_w': route_w, 'A': A, 'Bw': Bw}
    _L0_ffn_in = _L0_ffn_setup()
    _L0_c = _w((lambda *s: np.random.randn(*s).astype(np.float32) * 0.05)(1, 1024))
    _L0_wmod = _w((lambda *s: np.random.randn(*s).astype(np.float32) * 0.05)(1024, 6 * 1024) * 1024 ** (-0.5))
    _d = {'L0_attn_x': _L0_attn_in['x'], 'L0_attn_Wq': _L0_attn_in['Wq'], 'L0_attn_Wk': _L0_attn_in['Wk'], 'L0_attn_Wv': _L0_attn_in['Wv'], 'L0_attn_Wo': _L0_attn_in['Wo'], 'L0_ffn_route_w': _L0_ffn_in['route_w'], 'L0_ffn_A': _L0_ffn_in['A'], 'L0_ffn_Bw': _L0_ffn_in['Bw'], 'L0_c': _L0_c, 'L0_wmod': _L0_wmod}
    _x0 = _d['L0_attn_x']
    _d['L0_attn_x'] = jax.random.normal(jax.random.fold_in(jax.random.key(seed), 1), (1, 2048, 1024), dtype=_x0.dtype)
    del _x0
    return _d

def reference(L0_attn_x, L0_attn_Wq, L0_attn_Wk, L0_attn_Wv, L0_attn_Wo, L0_ffn_route_w, L0_ffn_A, L0_ffn_Bw, L0_c, L0_wmod):

    def _L0_attn_ref(x, Wq, Wk, Wv, Wo):
        import jax, jax.numpy as jnp
        import numpy as np
        import math
        B, T, D_IN, D_OUT = (2, 512, 1024, 1024)
        N_HEADS, N_KV = (32, 8)
        HEAD_DIM = D_OUT // N_HEADS
        GROUP_SIZE = N_HEADS // N_KV
        ROPE_BASE = 500000.0
        CTX = 512

        def _rope_tables(head_dim, base, seq_len):
            inv_freq = 1.0 / base ** (jnp.arange(0, head_dim, 2, dtype=jnp.float32) / head_dim)
            t = jnp.arange(seq_len, dtype=jnp.float32)
            freqs = jnp.einsum('i,j->ij', t, inv_freq)
            return (jnp.cos(freqs), jnp.sin(freqs))

        def _apply_rope(x, cos, sin):
            x1, x2 = jnp.split(x, 2, axis=-1)
            c = cos[None, None]
            s = sin[None, None]
            return jnp.concatenate([x1 * c - x2 * s, x1 * s + x2 * c], axis=-1)
        b, t, _ = x.shape
        cos, sin = _rope_tables(HEAD_DIM, ROPE_BASE, t)
        q = (x @ Wq).reshape(b, t, N_HEADS, HEAD_DIM).transpose(0, 2, 1, 3)
        k = (x @ Wk).reshape(b, t, N_KV, HEAD_DIM).transpose(0, 2, 1, 3)
        v = (x @ Wv).reshape(b, t, N_KV, HEAD_DIM).transpose(0, 2, 1, 3)
        q = _apply_rope(q, cos, sin)
        k = _apply_rope(k, cos, sin)
        k_h = jnp.repeat(k, GROUP_SIZE, axis=1)
        v_h = jnp.repeat(v, GROUP_SIZE, axis=1)
        scores = jnp.einsum('bhqd,bhkd->bhqk', q, k_h) / math.sqrt(HEAD_DIM)
        causal = jnp.triu(jnp.ones((t, t), dtype=bool), k=1)
        scores = jnp.where(causal[None, None], jnp.finfo(scores.dtype).min, scores)
        attn = jax.nn.softmax(scores, axis=-1)
        ctx = jnp.einsum('bhqk,bhkd->bhqd', attn, v_h)
        ctx = ctx.transpose(0, 2, 1, 3).reshape(b, t, D_OUT)
        return ctx @ Wo

    def _L0_ffn_ref(x, route_w, A, Bw):
        import jax, jax.numpy as jnp
        import numpy as np
        R = 16
        LORA_ALPHA = 16
        SCALING = LORA_ALPHA / R
        logits = jnp.einsum('bsd,ed->bse', x, route_w)
        topk_v, topk_idx = jax.lax.top_k(logits, 1)
        E = logits.shape[-1]
        route_weight = jax.nn.one_hot(topk_idx[..., 0], E, dtype=logits.dtype) * topk_v
        h = jnp.einsum('bsd,erd->bser', x, A)
        wh = route_weight[..., None] * h
        out = jnp.einsum('bser,eor->bso', wh, Bw) * SCALING
        return out
    x = L0_attn_x
    mod = (_silu(L0_c) @ L0_wmod).reshape(L0_c.shape[0], 6, 1, -1)
    sa, ca, ga, sb, cb, gb = (mod[:, 0], mod[:, 1], mod[:, 2], mod[:, 3], mod[:, 4], mod[:, 5])
    ga = (2 * (ga >= 0) - 1) * jnp.maximum(jnp.abs(ga), 0.25)
    gb = (2 * (gb >= 0) - 1) * jnp.maximum(jnp.abs(gb), 0.25)
    h = _layernorm(x, axis=-1) * (1 + ca) + sa
    x = x + ga * _L0_attn_ref(h, L0_attn_Wq, L0_attn_Wk, L0_attn_Wv, L0_attn_Wo)
    h = _layernorm(x, axis=-1) * (1 + cb) + sb
    x = x + gb * _L0_ffn_ref(h, L0_ffn_route_w, L0_ffn_A, L0_ffn_Bw)
    return x

_drawn_inputs = setup_inputs


def setup_inputs(seed=0):
    import zlib

    import numpy as np

    out = dict(_drawn_inputs(seed))
    spreads = {}
    factors = {'L0_attn_Wq': 8.0,
     'L0_attn_Wk': 8.0,
     'L0_attn_Wv': 8.0,
     'L0_attn_Wo': 8.0,
     'L0_ffn_route_w': 4.193,
     'L0_ffn_A': 3.624,
     'L0_ffn_Bw': 3.392,
     'L0_c': 3.087,
     'L0_wmod': 3.207}
    for name, (base, spread) in spreads.items():
        noise = np.random.default_rng([zlib.crc32(name.encode()), seed]).standard_normal(out[name].shape)
        drawn = base * np.exp(spread * noise) if base else spread * noise
        out[name] = jnp.asarray(drawn.astype(out[name].dtype))
    for name, factor in factors.items():
        out[name] = (out[name] * factor).astype(out[name].dtype)
    return out
```

```python
from contextlib import ExitStack

import numpy as np

import concourse.bass as bass
from concourse import mybir

F32 = mybir.dt.float32
F32R = mybir.dt.float32r
BF16 = mybir.dt.bfloat16
ALU = mybir.AluOpType
ACT = mybir.ActivationFunctionType
AX = mybir.AxisListType

P = 128
T, D = 2048, 1024
HEADS, KVH, HD = 32, 8, 32
GRP = HEADS // KVH
HALF = HD // 2
KT = D // P
CH = 512
NCH = T // CH
TPC = CH // P
NTT = T // P
EXPERTS, RANK = 8, 16
ER = EXPERTS * RANK
LN_EPS = 1e-5
SCORE_SCALE = float(HD) ** -0.5
MASKED = -1e30

KV_W = KVH * HD
COL_K, COL_V, COL_Q = 0, KV_W, 2 * KV_W
WCOLS = COL_Q + HEADS * HD
HPU = P // HALF
QUNITS = HEADS // HPU
UNITS = 2 + QUNITS
ROPES = 1 + QUNITS

MODC = 256
MPP = D // MODC


def wait_past(eng, sem, value):
    if not isinstance(value, int) or value > 0:
        eng.wait_ge(sem, value)


def modulate_block(nc, io, S, M):
    ctx = ExitStack()
    with ctx:
        def sb(name, shape, dt=F32):
            return ctx.enter_context(nc.sbuf_tensor(name, shape, dt))

        def sem(name):
            return ctx.enter_context(nc.semaphore(name))

        piece = sb("wmod_piece", [P, 2, KT, MODC])
        wraw = sb("w_raw", [P, 2, WCOLS])
        c_col = sb("c_col", [P, KT])
        c_exp = sb("c_exp", [P, KT])
        c_den = sb("c_den", [P, KT])
        c_rec = sb("c_rec", [P, KT])
        c_act = sb("c_act", [P, KT])
        c_wide = sb("c_wide", [P, KT, P])
        ones = sb("ones_wide", [P, P])
        g_row = sb("g_row", [1, 2, D])
        g_neg = sb("g_neg", [1, 2, D])
        g_abs = sb("g_abs", [1, 2, D])
        g_sgn = sb("g_sgn", [1, 2, D])
        g_fin = sb("g_fin", [1, 2, D])
        cols_ps = M["psum"][:, 0, :]
        gate_ps = M["psum"][:, 1:5, :].rearrange("p (g h) n -> p g (h n)", g=2)

        c_in = sem("c_in")
        const_in = sem("const_in")
        piece_in = [sem(f"piece_in{i}") for i in range(2)]
        piece_used = sem("piece_used")
        w_in = [sem(f"w_in{i}") for i in range(2)]
        w_hi_done = sem("w_hi_done")
        w_split = sem("w_split")
        exp_ready = sem("exp_ready")
        wide_ready = sem("wide_ready")
        gate_ready = sem("gate_ready")
        gate_out = sem("gate_out")
        chain = sem("mod_chain")
        block = ctx.enter_context(nc.Block())

        COLUMN_OF = {0: 0, 1: 1, 3: 2, 4: 3}
        GATE_OF = {2: 0, 5: 1}
        wmod_v = io["wmod"].rearrange("(p kk) n -> p kk n", kk=KT)

        @block.sync
        def _(sp):
            sp.dma_start(c_col[:], io["c"].rearrange("a (p kk) -> (a p) kk", kk=KT)).then_inc(c_in, 16)
            sp.dma_start(M["ident"][:], io["consts"][:, 0:P]).then_inc(const_in, 16)
            sp.dma_start(M["ranks"][:], io["consts"][:, P:P + EXPERTS]).then_inc(const_in, 16)
            sp.dma_start(M["masks"][:], io["masks"]).then_inc(const_in, 16)
            for n in range(6 * MPP):
                if n >= 2:
                    sp.wait_ge(piece_used, n - 1)
                sp.dma_start(piece[:, n % 2], wmod_v[:, :, n * MODC:(n + 1) * MODC]).then_inc(piece_in[n % 2], 16)
            sp.wait_ge(gate_ready, 1)
            sp.dma_start(S["gates"].rearrange("g n -> (g n)").rearrange("(a n) -> a n", a=1),
                         g_fin[0:1].rearrange("p g n -> p (g n)")).then_inc(gate_out, 16)
            sp.wait_ge(gate_out, 16)
            sp.wait_ge(const_in, 48)

        @block.scalar
        def _(act):
            def load(kt):
                if kt >= 2:
                    act.wait_ge(w_split, kt - 1)
                act.dma_start(wraw[:, kt % 2], io["wqkv"][kt * P:(kt + 1) * P, :]).then_inc(w_in[kt % 2], 16)

            load(0)
            load(1)
            act.wait_ge(c_in, 16)
            nc.scalar.activation(c_exp[:], c_col[:], ACT.Exp, scale=-1.0).then_inc(exp_ready, 1)
            for kt in range(KT):
                act.wait_ge(w_in[kt % 2], 16 * (kt // 2 + 1))
                nc.scalar.activation(M["w_hi"][:, kt], wraw[:, kt % 2], ACT.Copy).then_inc(w_hi_done, 1)
                if kt + 2 < KT:
                    load(kt + 2)

        @block.vector
        def _(dve):
            done = 0

            def link(ins):
                nonlocal done
                done += 1
                ins.then_inc(chain, 1)
                dve.wait_ge(chain, done)

            link(nc.vector.memset(ones[:], 1.0))
            dve.wait_ge(exp_ready, 1)
            link(nc.vector.tensor_scalar_add(c_den[:], c_exp[:], 1.0))
            link(nc.vector.reciprocal(c_rec[:], c_den[:]))
            link(nc.vector.tensor_tensor(c_act[:], c_col[:], c_rec[:], ALU.mult))
            for kk in range(KT):
                last = nc.vector.tensor_scalar(c_wide[:, kk], ones[:], c_act[:, kk:kk + 1], None, ALU.mult)
            last.then_inc(wide_ready, 1)
            for kt in range(KT):
                dve.wait_ge(w_hi_done, kt + 1)
                nc.vector.tensor_tensor(M["w_lo"][:, kt], wraw[:, kt % 2], M["w_hi"][:, kt].bitcast(F32),
                                        ALU.subtract).then_inc(w_split, 1)
            dve.wait_ge(piece_used, 6 * MPP)
            mod = M["mod"]
            nc.vector.tensor_copy(mod[:, 0, :], cols_ps[:, 0:KT])
            nc.vector.tensor_scalar_add(mod[:, 1, :], cols_ps[:, KT:2 * KT], 1.0)
            nc.vector.tensor_copy(mod[:, 2, :], cols_ps[:, 2 * KT:3 * KT])
            nc.vector.tensor_scalar_add(mod[:, 3, :], cols_ps[:, 3 * KT:4 * KT], 1.0)
            link(nc.vector.tensor_copy(g_row[0:1], gate_ps[0:1]))
            link(nc.vector.tensor_scalar(g_neg[0:1], g_row[0:1], -1.0, None, ALU.mult))
            link(nc.vector.tensor_tensor(g_abs[0:1], g_row[0:1], g_neg[0:1], ALU.max))
            link(nc.vector.tensor_scalar(g_sgn[0:1], g_row[0:1], 0.0, 2.0, ALU.is_ge, ALU.mult))
            link(nc.vector.tensor_scalar(g_neg[0:1], g_sgn[0:1], 1.0, None, ALU.subtract))
            link(nc.vector.tensor_scalar(g_sgn[0:1], g_abs[0:1], 0.25, None, ALU.max))
            nc.vector.tensor_tensor(g_fin[0:1], g_sgn[0:1], g_neg[0:1], ALU.mult).then_inc(gate_ready, 1)

        @block.tensor
        def _(pe):
            pe.wait_ge(wide_ready, 1)
            for n in range(6 * MPP):
                param, part = divmod(n, MPP)
                pe.wait_ge(piece_in[n % 2], 16 * (n // 2 + 1))
                if param in COLUMN_OF:
                    for half in range(MODC // P):
                        col = COLUMN_OF[param] * KT + part * (MODC // P) + half
                        for kk in range(KT):
                            last = nc.tensor.matmul(cols_ps[:, col:col + 1], piece[:, n % 2, kk, half * P:(half + 1) * P],
                                                    c_act[:, kk:kk + 1], start=(kk == 0), stop=(kk == KT - 1))
                else:
                    out = gate_ps[:, GATE_OF[param], part * MODC:(part + 1) * MODC]
                    for kk in range(KT):
                        last = nc.tensor.matmul(out, c_wide[:, kk], piece[:, n % 2, kk],
                                                start=(kk == 0), stop=(kk == KT - 1))
                last.then_inc(piece_used, 1)


def project_block(nc, io, S, M):
    ctx = ExitStack()
    with ctx:
        def sb(name, shape, dt=F32):
            return ctx.enter_context(nc.sbuf_tensor(name, shape, dt))

        def sem(name):
            return ctx.enter_context(nc.semaphore(name))

        x = sb("x_chunk", [P, TPC, D])
        xn = sb("x_normed", [P, TPC, D])
        hf = sb("h_full", [P, 2, CH])
        h_hi = sb("h_hi", [P, KT, CH], F32R)
        h_lo = sb("h_lo", [P, KT, CH], F32R)
        trig = sb("trig", [P, 2, CH])
        by_cos = sb("by_cos", [P, 2, CH])
        by_sin = sb("by_sin", [P, 2, CH])
        rot = sb("rotated", [P, 2, CH])
        rot_hi = sb("rotated_hi", [P, 2, CH], F32R)
        rot_lo = sb("rotated_lo", [P, 2, CH], F32R)
        stats = sb("ln_stats", [P, TPC, 2, 6])
        meanvar = sb("ln_meanvar", [P, TPC, 2])
        var = sb("ln_var", [P, TPC])
        std = sb("ln_std", [P, TPC])
        cell = sb("hold_cell", [P, 1])
        r0 = sb("ln_r0", [P, TPC])
        r1 = sb("ln_r1", [P, TPC])
        r2 = sb("ln_r2", [P, TPC])
        rstd = sb("ln_rstd", [P, TPC])
        w_hi, w_lo, ident, mod, v_all = M["w_hi"], M["w_lo"], M["ident"], M["mod"], M["v_all"]
        unit_ps = M["psum"][:, 0:4].rearrange("p (s b) n -> p s b n", s=2)
        tr_ps = M["psum"][:, 4:8]

        x_in = [sem(f"x_in{j}") for j in range(TPC)]
        trig_in = sem("trig_in")
        var_ready = sem("var_ready")
        std_ready = sem("std_ready")
        xn_ready = sem("xn_ready")
        tr_ready = sem("tr_ready")
        hf_ready = sem("hf_ready")
        hh_ready = sem("hh_ready")
        h_ready = sem("h_ready")
        unit_ready = sem("unit_ready")
        v_read = sem("v_read")
        rope_read = sem("rope_read")
        rot_ready = sem("rot_ready")
        hi_ready = sem("hi_ready")
        lo_ready = sem("lo_ready")
        hi_out = sem("hi_out")
        lo_out = sem("lo_out")
        chain = sem("proj_chain")
        block = ctx.enter_context(nc.Block())

        q_dram, k_dram = S["q"], S["k"]

        @block.sync
        def _(sp):
            def load_x(n, j):
                sp.dma_start(x[:, j], io["x"][bass.ds(n * CH + j * P, P), :]).then_inc(x_in[j], 16)

            def chunk(n, first, last):
                if not first:
                    sp.wait_ge(rope_read, n * ROPES)
                sp.dma_start(trig[:], io["trig"][:, :, bass.ds(n * CH, CH)]).then_inc(trig_in, 16)
                if not last:
                    for j in range(TPC):
                        sp.wait_ge(xn_ready, n * TPC + j + 1)
                        load_x(n + 1, j)
                for r in range(ROPES):
                    for part, tile, ready, out in ((0, rot_hi, hi_ready, hi_out), (1, rot_lo, lo_ready, lo_out)):
                        sp.wait_ge(ready, n * ROPES + r + 1)
                        for b in range(2):
                            heads = slice(0, KVH) if r == 0 else slice((r - 1) * HPU, r * HPU)
                            dst = (k_dram if r == 0 else q_dram)[part, b, heads, :, bass.ds(n * CH, CH)]
                            sp.dma_start(dst.rearrange("h i t -> (h i) t"), tile[:, b].bitcast(F32)).then_inc(out, 16)

            for j in range(TPC):
                load_x(0, j)
            chunk(0, True, False)
            with sp.Fori(1, NCH - 1) as n:
                chunk(n, False, False)
            chunk(NCH - 1, False, True)
            sp.wait_ge(hi_out, NCH * ROPES * 32)
            sp.wait_ge(lo_out, NCH * ROPES * 32)

        @block.scalar
        def _(act):
            def sqrt_of_var(n):
                act.wait_ge(var_ready, n + 1)
                nc.scalar.activation(std[:], var[:], ACT.Sqrt).then_inc(std_ready, 1)

            def rope_hi(n, r, first):
                act.wait_ge(rot_ready, n * ROPES + r + 1)
                if not (first and r == 0):
                    act.wait_ge(hi_out, (n * ROPES + r) * 32)
                nc.scalar.activation(rot_hi[:], rot[:], ACT.Copy).then_inc(hi_ready, 1)

            def chunk(n, first, last):
                for kt in range(KT):
                    act.wait_ge(tr_ready, n * KT + kt + 1)
                    if not (first and kt < 2):
                        act.wait_ge(h_ready, n * KT + kt - 1)
                    nc.scalar.activation(hf[:, kt % 2], tr_ps[:, kt % 4], ACT.Identity, bias=mod[:, 0, kt:kt + 1],
                                         scale=mod[:, 1, kt:kt + 1]).then_inc(hf_ready, 1)
                if not last:
                    sqrt_of_var(n + 1)
                rope_hi(n, 0, first)
                act.wait_ge(unit_ready, n * UNITS + 2)
                nc.scalar.activation(v_all[:, bass.ds(n * TPC, TPC), :], unit_ps[:, 1].rearrange("p b (j c) -> p (b j) c", j=2),
                                     ACT.Copy).then_inc(v_read, 1)
                for r in range(1, ROPES):
                    rope_hi(n, r, first)

            sqrt_of_var(0)
            chunk(0, True, False)
            with act.Fori(1, NCH - 1) as n:
                chunk(n, False, False)
            chunk(NCH - 1, False, True)

        @block.vector
        def _(dve):
            LINKS = TPC * 3 + 6

            def norm(n, first):
                base = n * LINKS
                k = 0

                def link(ins):
                    nonlocal k
                    k += 1
                    ins.then_inc(chain, 1)

                for j in range(TPC):
                    dve.wait_ge(x_in[j], (n + 1) * 16)
                    for half in range(2):
                        link(nc.vector.bn_stats(stats[:, j, half], x[:, j, half * CH:(half + 1) * CH]))
                dve.wait_ge(chain, base + k)
                link(nc.vector.tensor_copy(cell[:], ident[:, 0:1]))
                for j in range(TPC):
                    link(nc.vector.bn_aggr(meanvar[:, j], stats[:, j]))
                dve.wait_ge(chain, base + k)
                nc.vector.tensor_scalar_add(var[:], meanvar[:, :, 1], LN_EPS).then_inc(var_ready, 1)
                dve.wait_ge(std_ready, n + 1)
                link(nc.vector.reciprocal(r0[:], std[:]))
                dve.wait_ge(chain, base + k)
                link(nc.vector.tensor_tensor(r1[:], r0[:], r0[:], ALU.mult))
                dve.wait_ge(chain, base + k)
                link(nc.vector.tensor_tensor(r2[:], r1[:], var[:], ALU.mult))
                dve.wait_ge(chain, base + k)
                link(nc.vector.tensor_scalar(r1[:], r2[:], -0.5, 1.5, ALU.mult, ALU.add))
                dve.wait_ge(chain, base + k)
                link(nc.vector.tensor_tensor(rstd[:], r0[:], r1[:], ALU.mult))
                dve.wait_ge(chain, base + k)
                assert k == LINKS
                if not first:
                    dve.wait_ge(tr_ready, n * KT)
                for j in range(TPC):
                    nc.vector.tensor_scalar(xn[:, j], x[:, j], meanvar[:, j, 0:1], rstd[:, j:j + 1],
                                            ALU.subtract, ALU.mult).then_inc(xn_ready, 1)

            def split_lo(n, r, first):
                dve.wait_ge(hi_ready, n * ROPES + r + 1)
                if not (first and r == 0):
                    dve.wait_ge(lo_out, (n * ROPES + r) * 32)
                nc.vector.tensor_tensor(rot_lo[:], rot[:], rot_hi[:].bitcast(F32), ALU.subtract).then_inc(lo_ready, 1)

            def chunk(n, first, last):
                for kt in range(KT):
                    dve.wait_ge(hf_ready, n * KT + kt + 1)
                    if not first and kt == 0:
                        dve.wait_ge(unit_ready, n * UNITS)
                    nc.vector.tensor_copy(h_hi[:, kt], hf[:, kt % 2]).then_inc(hh_ready, 1)
                    dve.wait_ge(hh_ready, n * KT + kt + 1)
                    nc.vector.tensor_tensor(h_lo[:, kt], hf[:, kt % 2], h_hi[:, kt].bitcast(F32),
                                            ALU.subtract).then_inc(h_ready, 1)
                if not last:
                    norm(n + 1, False)
                dve.wait_ge(trig_in, (n + 1) * 16)
                for r in range(ROPES):
                    unit = 0 if r == 0 else r + 1
                    dve.wait_ge(unit_ready, n * UNITS + unit + 1)
                    if not (first and r == 0):
                        dve.wait_ge(rot_ready, n * ROPES + r)
                    for tile, f in ((by_cos, 0), (by_sin, 1)):
                        table = trig[:, f:f + 1, :].broadcast_to((P, 2, CH))
                        last_ins = nc.vector.tensor_tensor(tile[:], unit_ps[:, unit % 2], table, ALU.mult)
                    last_ins.then_inc(rope_read, 1)
                    if r:
                        split_lo(n, r - 1, first)
                split_lo(n, ROPES - 1, False)

            norm(0, True)
            chunk(0, True, False)
            with dve.Fori(1, NCH - 1) as n:
                chunk(n, False, False)
            chunk(NCH - 1, False, True)

        @block.gpsimd
        def _(pool):
            def chunk(n, first):
                for r in range(ROPES):
                    pool.wait_ge(rope_read, n * ROPES + r + 1)
                    if not (first and r == 0):
                        pool.wait_ge(lo_ready, n * ROPES + r)
                    nc.gpsimd.tensor_tensor(rot[:, 0], by_cos[:, 0], by_sin[:, 1], ALU.subtract)
                    nc.gpsimd.tensor_tensor(rot[:, 1], by_sin[:, 0], by_cos[:, 1], ALU.add).then_inc(rot_ready, 1)

            chunk(0, True)
            with pool.Fori(1, NCH) as n:
                chunk(n, False)

        @block.tensor
        def _(pe):
            def products(out, terms, start, stop):
                for i, (lhs, rhs) in enumerate(terms):
                    last = nc.tensor.matmul(out, lhs, rhs, start=start and i == 0, stop=stop and i == len(terms) - 1)
                return last

            def chunk(n, first):
                pe.wait_ge(xn_ready, (n + 1) * TPC)
                for kt in range(KT):
                    if not (first and kt < 4):
                        pe.wait_ge(hf_ready, n * KT + kt - 3)
                    for j in range(TPC):
                        last = nc.tensor.transpose(tr_ps[:, kt % 4, j * P:(j + 1) * P], xn[:, j, kt * P:(kt + 1) * P], ident[:])
                    last.then_inc(tr_ready, 1)
                for unit in range(UNITS):
                    if unit == 3:
                        pe.wait_ge(v_read, n + 1)
                    elif not (first and unit < 2):
                        pe.wait_ge(rope_read, n * ROPES + {0: -1, 1: 0, 2: 1, 4: 2, 5: 3}[unit])
                    if unit == 1:
                        for j in range(TPC):
                            out = unit_ps[:, 1, j // 2, (j % 2) * KV_W:(j % 2 + 1) * KV_W]
                            rows, cols = slice(j * P, (j + 1) * P), slice(COL_V, COL_V + KV_W)
                            for kt in range(KT):
                                last = products(out, ((h_hi[:, kt, rows], w_hi[:, kt, cols]), (h_hi[:, kt, rows], w_lo[:, kt, cols]),
                                                      (h_lo[:, kt, rows], w_hi[:, kt, cols])), kt == 0, kt == KT - 1)
                    else:
                        at = COL_K if unit == 0 else COL_Q + (unit - 2) * 2 * P
                        for kt in range(KT):
                            if unit == 0:
                                pe.wait_ge(h_ready, n * KT + kt + 1)
                            for b in range(2):
                                cols = slice(at + b * P, at + (b + 1) * P)
                                last = products(unit_ps[:, unit % 2, b], ((w_hi[:, kt, cols], h_hi[:, kt]), (w_hi[:, kt, cols], h_lo[:, kt]),
                                                                          (w_lo[:, kt, cols], h_hi[:, kt])), kt == 0, kt == KT - 1)
                    last.then_inc(unit_ready, 1)

            chunk(0, True)
            with pe.Fori(1, NCH) as n:
                chunk(n, False)


def attend_block(nc, io, S, M):
    ctx = ExitStack()
    with ctx:
        def sb(name, shape, dt=F32):
            return ctx.enter_context(nc.sbuf_tensor(name, shape, dt))

        def sem(name):
            return ctx.enter_context(nc.semaphore(name))

        NP = 4
        ONES_ROW = 3 * HD
        qs = [sb(f"q_stack{u}", [ONES_ROW + 1, GRP, T], F32R) for u in range(2)]
        ks = [sb(f"k_stack{u}", [ONES_ROW + 1, T], F32R) for u in range(2)]
        v_g = [sb(f"v_group{u}", [P, NTT, HD]) for u in range(2)]
        probs = sb("probs", [P, NP, GRP, CH])
        part_max = sb("part_max", [P, NTT, GRP, NCH])
        q_max = sb("q_max", [P, 2, GRP, NTT])
        neg_max = sb("neg_max", [GRP * NTT, P], F32R)
        ones = sb("ones_sum", [P, HD])
        o_raw = sb("o_raw", [P, CH])
        o_sum = sb("o_sum", [P, CH])
        o_rec = sb("o_rec", [P, CH])
        o_full = sb("o_full", [P, CH])
        o_hi = sb("o_hi", [P, CH], F32R)
        o_lo = sb("o_lo", [P, CH], F32R)
        ident, masks, v_all = M["ident"], M["masks"], M["v_all"]
        ident_b, mask_qk, mask_kq = masks[:, 0], masks[:, 1], masks[:, 2]
        max_ps = M["psum"][:, 0:4].rearrange("p (s b) n -> p s b n", s=2)
        score_ps = M["psum"][:, 4:6]
        out_ps = M["psum"][:, 6]
        sum_ps = M["psum"][:, 7]

        STEPS = [(c, kb) for c in range(NCH) for kb in range((c + 1) * TPC)]
        LAST = [max(n for n, st in enumerate(STEPS) if st[0] == c) for c in range(NCH)]
        MAXES = [(qb, kc, hp) for qb in range(NTT) for kc in range(qb // TPC + 1) for hp in range(2)]
        NS, NM = len(STEPS), len(MAXES)
        FROM, TO = 5, 36
        LOADS = 12
        LAG = 2

        load_in = [sem(f"load_in{u}") for u in range(2)]
        negmax_in = [sem(f"negmax_in{u}") for u in range(2)]
        ones_ready = sem("ones_ready")
        v_ready = sem("v_ready")
        score_ready = sem("score_ready")
        prob_ready = sem("prob_ready")
        step_done = sem("step_done")
        max_ready = sem("max_ready")
        max_read = sem("max_read")
        qmax_ready = sem("qmax_ready")
        maxt_ready = sem("maxt_ready")
        negmax_ready = sem("negmax_ready")
        raw_ready = sem("raw_ready")
        rec_ready = sem("rec_ready")
        o_ready = sem("o_ready")
        hi_ready = sem("o_hi_ready")
        split_ready = sem("o_split_ready")
        o_out = sem("o_out")
        block = ctx.enter_context(nc.Block())

        def passes(eng, one):
            one(0, 0, False, True)
            one(0, 0, True, True)
            with eng.Fori(0, (KVH - 2) // 2) as i:
                one(i, 1, True, True)
                one(i + 1, 0, True, True)
            one(KVH // 2 - 1, 1, True, False)

        def after(h, u, weigh):
            if not weigh:
                return h, u
            return (h, 1) if u == 0 else (h + 1, 0)

        def schedule(weigh, maxima):
            if not weigh:
                return [list(range(NM + 1))]
            out = [[] for _ in STEPS]
            if maxima:
                size = [min(CH, (qb + 1) * P - kc * CH) for qb, kc, hp in MAXES]
                seen = 0
                for m in range(NM):
                    out[FROM + (TO - FROM) * seen // sum(size)].append(m)
                    seen += size[m]
                out[TO].append(NM)
            return out

        @block.sync
        def _(sp):
            def store(s, c):
                sp.wait_ge(split_ready, s * NCH + c + 1)
                for part, tile in ((0, o_hi), (1, o_lo)):
                    sp.dma_start(S["o"][part, bass.ds(s, 1), :, c * CH:(c + 1) * CH].rearrange("a p t -> (a p) t"),
                                 tile[:].bitcast(F32)).then_inc(o_out, 16)

            def one(h, u, weigh, maxima):
                s = h * 2 + u
                gh, v = after(h, u, weigh)
                g = gh * 2 + v
                if maxima:
                    wait_past(sp, step_done, s * NS)
                    for block_of_rows, q_part, k_part in ((0, 0, 0), (1, 0, 1), (2, 1, 0)):
                        for b in range(2):
                            at = block_of_rows * HD + b * HALF
                            sp.dma_start(ks[v][at:at + HALF].bitcast(F32),
                                         S["k"][k_part, b, bass.ds(g, 1)].rearrange("a i t -> (a i) t")).then_inc(load_in[v], 16)
                            sp.dma_start(qs[v][at:at + HALF].bitcast(F32),
                                         S["q"][q_part, b, bass.ds(g * GRP, GRP)].rearrange("j i t -> i j t")).then_inc(load_in[v], 16)
                if weigh:
                    if not isinstance(s, int) or s > 0:
                        store(s - 1, NCH - 1)
                    for c in range(NCH - 1):
                        store(s, c)
                if maxima:
                    sp.wait_ge(negmax_ready, g + 1)
                    sp.dma_start(qs[v][ONES_ROW:ONES_ROW + 1].bitcast(F32)
                                 .rearrange("a j (b t) -> a (j b) t", t=P), neg_max[:].bitcast(F32)).then_inc(negmax_in[v], 16)

            passes(sp, one)
            store(KVH - 1, NCH - 1)
            sp.wait_ge(o_out, KVH * NCH * 32)

        @block.scalar
        def _(act):
            def one(h, u, weigh, maxima):
                s = h * 2 + u

                def copy_out(c):
                    act.wait_ge(step_done, s * NS + LAST[c] + 1)
                    wait_past(act, o_ready, s * NCH + c)
                    nc.scalar.activation(o_sum[:], sum_ps, ACT.Copy)
                    nc.scalar.activation(o_raw[:], out_ps, ACT.Copy).then_inc(raw_ready, 1)

                if not weigh:
                    return
                for n, (c, kb) in enumerate(STEPS):
                    off = max(0, kb * P - c * CH)
                    wait_past(act, step_done, s * NS + n - NP + 1)
                    for j in range(GRP):
                        act.wait_ge(score_ready, (s * NS + n) * GRP + j + 1)
                        nc.scalar.activation(probs[:, n % NP, j, off:], score_ps[:, j % 2, off:], ACT.Exp,
                                             scale=SCORE_SCALE).then_inc(prob_ready, 1)
                        if j == 1 and n - LAG in LAST:
                            copy_out(STEPS[n - LAG][0])
                copy_out(NCH - 1)

            assert NS % NP == 0
            passes(act, one)

        @block.gpsimd
        def _(pool):
            nc.gpsimd.memset(ones[:], 1.0).then_inc(ones_ready, 1)
            nc.gpsimd.memset(q_max[:, 1], 0.0).then_inc(ones_ready, 1)
            for v in range(2):
                pool.wait_ge(ones_ready, v + 2)
                nc.gpsimd.memset(ks[v][ONES_ROW:ONES_ROW + 1].bitcast(F32), 1.0).then_inc(ones_ready, 1)

            def one(h, u, weigh, maxima):
                s = h * 2 + u
                if not weigh:
                    return
                for c in range(NCH):
                    pool.wait_ge(hi_ready, s * NCH + c + 1)
                    nc.gpsimd.tensor_tensor(o_lo[:], o_full[:], o_hi[:].bitcast(F32), ALU.subtract).then_inc(split_ready, 1)

            passes(pool, one)

        @block.vector
        def _(dve):
            def one(h, u, weigh, maxima):
                s = h * 2 + u
                gh, v = after(h, u, weigh)
                g = gh * 2 + v
                plan = schedule(weigh, maxima)

                def values_of_group():
                    wait_past(dve, step_done, s * NS)
                    nc.vector.tensor_copy(v_g[v][:], v_all[:, :, bass.ds(g * HD, HD)]).then_inc(v_ready, 1)

                def take_max(m):
                    if m == NM:
                        dve.wait_ge(maxt_ready, g + 1)
                        if weigh:
                            dve.wait_ge(negmax_in[1 - v], (gh + v) * 16)
                        nc.vector.tensor_scalar(neg_max[:], max_ps[0:GRP * NTT, 0, 0, 0:P], -1.0, None,
                                                ALU.mult).then_inc(negmax_ready, 1)
                        return
                    dve.wait_ge(max_ready, g * NM + m + 1)
                    qb, kc, hp = MAXES[m]
                    w = min(CH, (qb + 1) * P - kc * CH)
                    nc.vector.tensor_reduce(part_max[:, qb, 2 * hp:2 * hp + 2, kc], max_ps[:, m % 2, :, 0:w],
                                            op=ALU.max, axis=AX.X).then_inc(max_read, 1)
                    if m == NM - 1:
                        dve.wait_ge(max_read, g * NM + NM)
                        for c in range(NCH):
                            tiles = slice(c * TPC, (c + 1) * TPC)
                            last = nc.vector.tensor_reduce(q_max[:, 0, :, tiles].rearrange("p j b -> p b j"), part_max[:, tiles, :, 0:c + 1],
                                                           op=ALU.max, axis=AX.X)
                        last.then_inc(qmax_ready, 1)

                def normalise(c, q):
                    cols = slice(q * P, (q + 1) * P)
                    if q == 0:
                        dve.wait_ge(raw_ready, s * NCH + c + 1)
                        wait_past(dve, split_ready, s * NCH + c)
                        wait_past(dve, o_out, (s * NCH + c) * 32)
                    nc.vector.reciprocal(o_rec[:, cols], o_sum[:, cols]).then_inc(rec_ready, 1)
                    dve.wait_ge(rec_ready, (s * NCH + c) * TPC + q + 1)
                    ins = nc.vector.tensor_tensor(o_full[:, cols], o_raw[:, cols], o_rec[:, cols], ALU.mult)
                    if q == TPC - 1:
                        ins.then_inc(o_ready, 1)
                        dve.wait_ge(o_ready, s * NCH + c + 1)
                        nc.vector.tensor_copy(o_hi[:], o_full[:]).then_inc(hi_ready, 1)

                if not weigh:
                    values_of_group()
                    for m in plan[0]:
                        take_max(m)
                    return
                for n in range(NS):
                    if n == FROM and maxima:
                        values_of_group()
                    for q in range(TPC):
                        if n - LAG - 1 - q in LAST:
                            normalise(STEPS[n - LAG - 1 - q][0], q)
                    for m in plan[n]:
                        take_max(m)
                for q in range(TPC):
                    normalise(NCH - 1, q)

            passes(dve, one)

        @block.tensor
        def _(pe):
            pe.wait_ge(ones_ready, 4)

            def one(h, u, weigh, maxima):
                s = h * 2 + u
                gh, v = after(h, u, weigh)
                g = gh * 2 + v
                plan = schedule(weigh, maxima)

                def max_unit(m):
                    if m == NM:
                        pe.wait_ge(qmax_ready, g + 1)
                        nc.tensor.transpose(max_ps[:, 0, 0, 0:P], q_max[:].rearrange("p z j b -> p (z j b)"),
                                            ident[:]).then_inc(maxt_ready, 1)
                        return
                    if m == 0:
                        pe.wait_ge(load_in[v], (gh + 1) * LOADS * 16)
                        wait_past(pe, negmax_ready, g)
                    if m >= 2:
                        pe.wait_ge(max_read, g * NM + m - 1)
                    qb, kc, hp = MAXES[m]
                    w = min(CH, (qb + 1) * P - kc * CH)
                    diag = kc == qb // TPC
                    for b in range(2):
                        last = nc.tensor.matmul(max_ps[:, m % 2, b, 0:w], qs[v][0:ONES_ROW, 2 * hp + b, qb * P:(qb + 1) * P],
                                                ks[v][0:ONES_ROW, kc * CH:kc * CH + w], start=True, stop=not diag)
                        if diag:
                            last = nc.tensor.matmul(max_ps[:, m % 2, b, w - P:w], ident_b, mask_qk, start=False, stop=True)
                    last.then_inc(max_ready, 1)

                if not weigh:
                    for m in plan[0]:
                        max_unit(m)
                    return

                def scores(n, heads):
                    c, kb = STEPS[n]
                    off = max(0, kb * P - c * CH)
                    diag = kb * P >= c * CH
                    for j in heads:
                        wait_past(pe, prob_ready, (s * NS + n) * GRP + j - 1)
                        last = nc.tensor.matmul(score_ps[:, j % 2, off:], ks[u][:, kb * P:(kb + 1) * P],
                                                qs[u][:, j, c * CH + off:(c + 1) * CH], start=True, stop=not diag)
                        if diag:
                            last = nc.tensor.matmul(score_ps[:, j % 2, off:off + P], ident_b, mask_kq, start=False, stop=True)
                        last.then_inc(score_ready, 1)

                def values(n):
                    c, kb = STEPS[n]
                    off = max(0, kb * P - c * CH)
                    if kb == 0:
                        wait_past(pe, raw_ready, s * NCH + c)
                    pe.wait_ge(prob_ready, (s * NS + n + 1) * GRP)
                    for lhs, out in ((v_g[u][:, kb], out_ps), (ones[:], sum_ps)):
                        for j in range(GRP):
                            last = nc.tensor.matmul(out[j * HD:(j + 1) * HD, off:], lhs, probs[:, n % NP, j, off:],
                                                    start=(kb == 0), stop=n in LAST)
                    last.then_inc(step_done, 1)

                pe.wait_ge(v_ready, s + 1)
                pe.wait_ge(negmax_in[u], (h + 1) * 16)
                for n in range(NS + LAG):
                    if n < NS:
                        scores(n, (0, 1))
                    if n >= LAG:
                        values(n - LAG)
                    if n < NS:
                        scores(n, (2, 3))
                        for m in plan[n]:
                            max_unit(m)

            passes(pe, one)


def feed_block(nc, io, S, M):
    ctx = ExitStack()
    with ctx:
        def sb(name, shape, dt=F32):
            return ctx.enter_context(nc.sbuf_tensor(name, shape, dt))

        def sem(name):
            return ctx.enter_context(nc.semaphore(name))

        RING = 4
        wo_hi = sb("wo_hi", [P, KT, D], F32R)
        wo_lo = sb("wo_lo", [P, KT, D], F32R)
        wo_raw = sb("wo_raw", [P, 2, D])
        down = sb("router_and_a", [P, KT, EXPERTS + ER])
        up = sb("lora_b", [P, D])
        gates = sb("gates", [P, 2, D])
        o_hi = sb("att_hi", [P, 2, KVH, P], F32R)
        o_lo = sb("att_lo", [P, 2, KVH, P], F32R)
        x_t = sb("x_tile", [P, 2, D])
        gated = sb("gated", [P, D])
        x1 = sb("x_mid", [P, RING, D])
        xn = sb("x_mid_normed", [P, D])
        h_t = sb("h_transposed", [P, KT, P])
        cell = sb("hold_cell2", [P, 1])
        top = sb("top_logit", [P, 1])
        top_rank = sb("top_rank", [P, 1])
        rank = sb("rank_where_top", [P, EXPERTS])
        route = sb("route_weight", [P, EXPERTS])
        wh = sb("weighted_h", [P, ER])
        wh_t = sb("weighted_h_t", [P, P])
        lora = sb("lora_gated", [P, D])
        y = sb("y_tile", [P, 2, D])
        stats = sb("ln2_stats", [P, 2, 6])
        meanvar = sb("ln2_meanvar", [P, 2])
        var = sb("ln2_var", [P, 1])
        std = sb("ln2_std", [P, 1])
        r0 = sb("ln2_r0", [P, 1])
        r1 = sb("ln2_r1", [P, 1])
        r2 = sb("ln2_r2", [P, 1])
        rstd = sb("ln2_rstd", [P, 1])
        ident, mod, ranks = M["ident"], M["mod"], M["ranks"]
        proj_ps = M["psum"][:, 0:2]
        tr_ps = M["psum"][:, 2:4].rearrange("p b (k t) -> p (b k) t", t=P)
        down_ps = M["psum"][:, 4]
        wht_ps = M["psum"][:, 5, 0:P]
        up_ps = M["psum"][:, 6:8]

        wo_in = [sem(f"wo_in{i}") for i in range(2)]
        wo_hi_ready = sem("wo_hi_ready")
        wo_split = sem("wo_split")
        small_in = sem("small_in")
        o_in = [sem(f"att_in{i}") for i in range(2)]
        x_in = [sem(f"x_tile_in{i}") for i in range(2)]
        y_out = [sem(f"y_out{i}") for i in range(2)]
        proj_ready = sem("proj_ready")
        proj_read = sem("proj_read")
        x1_ready = sem("x1_ready")
        var_ready = sem("var2_ready")
        std_ready = sem("std2_ready")
        xn_ready = sem("xn2_ready")
        tr_ready = sem("tr2_ready")
        h_ready = sem("h2_ready")
        down_ready = sem("down_ready")
        wh_ready = sem("wh_ready")
        wht_ready = sem("wht_ready")
        wht_read = sem("wht_read")
        up_ready = sem("up_ready")
        up_read = sem("up_read")
        y_ready = sem("y_ready")
        chain0, chain1 = sem("norm_chain"), sem("route_chain")
        block = ctx.enter_context(nc.Block())

        def steps(eng, step):
            for t in range(RING):
                step(t, t, t // 2, True, t >= 1, t >= 2)
            with eng.Fori(1, NTT // RING) as i:
                for r in range(RING):
                    step(i * RING + r, r, i * (RING // 2) + r // 2, True, True, True)
            step(NTT, 0, NTT // 2, False, True, True)
            step(NTT + 1, 1, NTT // 2, False, False, True)

        @block.sync
        def _(sp):
            def step(t, r, pairs, has0, has1, has2):
                if has0:
                    wait_past(sp, proj_ready, (t - 1) * 2)
                    for part, tile in ((0, o_hi), (1, o_lo)):
                        sp.dma_start(tile[:, r % 2].bitcast(F32), S["o"][part, :, :, bass.ds(t * P, P)].rearrange("g p t -> p g t"))\
                          .then_inc(o_in[r % 2], 16)
                    wait_past(sp, x1_ready, (t - 1) * 2)
                    sp.dma_start(x_t[:, r % 2], io["x"][bass.ds(t * P, P), :]).then_inc(x_in[r % 2], 16)
                if has2:
                    sp.wait_ge(y_ready, t - 1)
                    sp.dma_start(io["out"][bass.ds((t - 2) * P, P), :], y[:, r % 2]).then_inc(y_out[r % 2], 16)

            steps(sp, step)
            for i in range(2):
                sp.wait_ge(y_out[i], NTT // 2 * 16)

        @block.scalar
        def _(act):
            act.dma_start(gates[:], S["gates"].partition_broadcast(P)).then_inc(small_in, 16)
            act.dma_start(down[:], io["down"].rearrange("(k p) n -> p k n", p=P)).then_inc(small_in, 16)
            act.dma_start(up[:], io["up"]).then_inc(small_in, 16)

            def load(kt):
                wait_past(act, wo_split, kt - 1)
                act.dma_start(wo_raw[:, kt % 2], io["wo"][kt * P:(kt + 1) * P, :]).then_inc(wo_in[kt % 2], 16)

            load(0)
            load(1)
            for kt in range(KT):
                act.wait_ge(wo_in[kt % 2], 16 * (kt // 2 + 1))
                nc.scalar.activation(wo_hi[:, kt], wo_raw[:, kt % 2], ACT.Copy).then_inc(wo_hi_ready, 1)
                if kt + 2 < KT:
                    load(kt + 2)

            def step(t, r, pairs, has0, has1, has2):
                if has2:
                    act.wait_ge(wht_ready, t - 1)
                    wait_past(act, up_ready, t - 2)
                    nc.scalar.activation(wh_t[:], wht_ps, ACT.Copy).then_inc(wht_read, 1)
                if has1:
                    act.wait_ge(tr_ready, t)
                    wait_past(act, down_ready, t - 1)
                    for kt in range(KT):
                        last = nc.scalar.activation(h_t[:, kt], tr_ps[:, kt], ACT.Identity, bias=mod[:, 2, kt:kt + 1],
                                                    scale=mod[:, 3, kt:kt + 1])
                    last.then_inc(h_ready, 1)
                if has0:
                    act.wait_ge(var_ready, t + 1)
                    nc.scalar.activation(std[:], var[:], ACT.Sqrt).then_inc(std_ready, 1)

            steps(act, step)

        @block.vector
        def _(dve):
            for kt in range(KT):
                dve.wait_ge(wo_hi_ready, kt + 1)
                nc.vector.tensor_tensor(wo_lo[:, kt], wo_raw[:, kt % 2], wo_hi[:, kt].bitcast(F32),
                                        ALU.subtract).then_inc(wo_split, 1)
            dve.wait_ge(small_in, 48)
            NORM_LINKS, ROUTE_LINKS = 9, 4

            class Chain:

                def __init__(self, which, base):
                    self.which, self.base, self.k = which, base, 0

                def link(self, ins):
                    self.k += 1
                    ins.then_inc(self.which, 1)

                def wait(self):
                    dve.wait_ge(self.which, self.base + self.k)

            def residual(t, r, pairs, half, norm):
                cols = slice(half * CH, (half + 1) * CH)
                dve.wait_ge(proj_ready, t * 2 + half + 1)
                if half == 0:
                    dve.wait_ge(x_in[r % 2], (pairs + 1) * 16)
                nc.vector.tensor_tensor(gated[:, cols], proj_ps[:, half], gates[:, 0, cols], ALU.mult).then_inc(proj_read, 1)
                dve.wait_ge(proj_read, t * 2 + half + 1)
                nc.vector.tensor_tensor(x1[:, r, cols], gated[:, cols], x_t[:, r % 2, cols], ALU.add).then_inc(x1_ready, 1)
                dve.wait_ge(x1_ready, t * 2 + half + 1)
                norm.link(nc.vector.bn_stats(stats[:, half], x1[:, r, cols]))

            def finish_norm(t, r, norm):
                norm.wait()
                norm.link(nc.vector.tensor_copy(cell[:], ident[:, 0:1]))
                norm.link(nc.vector.bn_aggr(meanvar[:], stats[:]))
                norm.wait()
                nc.vector.tensor_scalar_add(var[:], meanvar[:, 1:2], LN_EPS).then_inc(var_ready, 1)
                dve.wait_ge(std_ready, t + 1)
                norm.link(nc.vector.reciprocal(r0[:], std[:]))
                norm.wait()
                norm.link(nc.vector.tensor_tensor(r1[:], r0[:], r0[:], ALU.mult))
                norm.wait()
                norm.link(nc.vector.tensor_tensor(r2[:], r1[:], var[:], ALU.mult))
                norm.wait()
                norm.link(nc.vector.tensor_scalar(r1[:], r2[:], -0.5, 1.5, ALU.mult, ALU.add))
                norm.wait()
                norm.link(nc.vector.tensor_tensor(rstd[:], r0[:], r1[:], ALU.mult))
                norm.wait()
                assert norm.k == NORM_LINKS
                wait_past(dve, tr_ready, t)
                nc.vector.tensor_scalar(xn[:], x1[:, r], meanvar[:, 0:1], rstd[:], ALU.subtract, ALU.mult).then_inc(xn_ready, 1)

            def route_tile(t):
                c = Chain(chain1, t * ROUTE_LINKS)
                dve.wait_ge(down_ready, t + 1)
                logits = down_ps[:, 0:EXPERTS]
                c.link(nc.vector.tensor_reduce(top[:], logits, op=ALU.max, axis=AX.X))
                c.wait()
                c.link(nc.vector.scalar_tensor_tensor(out=rank[:], in0=logits, scalar=top[:], in1=ranks[:],
                                                      op0=ALU.is_equal, op1=ALU.mult))
                c.wait()
                c.link(nc.vector.tensor_reduce(top_rank[:], rank[:], op=ALU.max, axis=AX.X))
                c.wait()
                c.link(nc.vector.tensor_scalar(route[:], rank[:], top_rank[:], top[:], ALU.is_equal, ALU.mult))
                c.wait()
                assert c.k == ROUTE_LINKS
                wait_past(dve, wht_ready, t)
                nc.vector.tensor_tensor(wh[:].rearrange("p (e r) -> p e r", r=RANK),
                                        down_ps[:, EXPERTS:EXPERTS + ER].rearrange("p (e r) -> p e r", r=RANK),
                                        route[:].rearrange("p (e a) -> p e a", a=1).broadcast_to((P, EXPERTS, RANK)),
                                        ALU.mult).then_inc(wh_ready, 1)

            def output(t, r, pairs):
                dve.wait_ge(up_ready, t + 1)
                nc.vector.tensor_tensor(lora[:].rearrange("p (b n) -> p b n", b=2), up_ps,
                                        gates[:, 1].rearrange("p (b n) -> p b n", b=2), ALU.mult).then_inc(up_read, 1)
                dve.wait_ge(up_read, t + 1)
                wait_past(dve, y_out[r % 2], pairs * 16)
                nc.vector.tensor_tensor(y[:, r % 2], lora[:], x1[:, r], ALU.add).then_inc(y_ready, 1)

            def step(t, r, pairs, has0, has1, has2):
                norm = Chain(chain0, t * NORM_LINKS)
                if has0:
                    residual(t, r, pairs, 0, norm)
                if has2:
                    output(t - 2, (r - 2) % RING, pairs - 1)
                if has0:
                    residual(t, r, pairs, 1, norm)
                if has1:
                    route_tile(t - 1)
                if has0:
                    finish_norm(t, r, norm)

            steps(dve, step)

        @block.tensor
        def _(pe):
            def project(t, r, pairs, half):
                cols = slice(half * CH, (half + 1) * CH)
                if half == 0:
                    pe.wait_ge(o_in[r % 2], (pairs + 1) * 32)
                wait_past(pe, proj_read, (t - 1) * 2 + half + 1)
                for g in range(KVH):
                    if isinstance(t, int) and t == 0 and half == 0:
                        pe.wait_ge(wo_split, g + 1)
                    terms = ((o_hi[:, r % 2, g], wo_hi[:, g, cols]), (o_hi[:, r % 2, g], wo_lo[:, g, cols]),
                             (o_lo[:, r % 2, g], wo_hi[:, g, cols]))
                    for i, (lhs, rhs) in enumerate(terms):
                        last = nc.tensor.matmul(proj_ps[:, half], lhs, rhs, start=g == 0 and i == 0, stop=g == KVH - 1 and i == 2)
                last.then_inc(proj_ready, 1)

            def step(t, r, pairs, has0, has1, has2):
                if has0:
                    project(t, r, pairs, 0)
                if has2:
                    pe.wait_ge(wh_ready, t - 1)
                    wait_past(pe, wht_read, t - 2)
                    nc.tensor.transpose(wht_ps, wh[:], ident[:]).then_inc(wht_ready, 1)
                if has1:
                    pe.wait_ge(xn_ready, t)
                    wait_past(pe, h_ready, t - 1)
                    for kt in range(KT):
                        last = nc.tensor.transpose(tr_ps[:, kt], xn[:, kt * P:(kt + 1) * P], ident[:])
                    last.then_inc(tr_ready, 1)
                if has2:
                    if isinstance(t, int) and t == 2:
                        pe.wait_ge(small_in, 48)
                    pe.wait_ge(wht_read, t - 1)
                    wait_past(pe, up_read, t - 2)
                    for b in range(2):
                        last = nc.tensor.matmul(up_ps[:, b], wh_t[:], up[:, b * CH:(b + 1) * CH], start=True, stop=True)
                    last.then_inc(up_ready, 1)
                if has0:
                    project(t, r, pairs, 1)
                if has1:
                    if isinstance(t, int) and t == 1:
                        pe.wait_ge(small_in, 48)
                    pe.wait_ge(h_ready, t)
                    wait_past(pe, wh_ready, t - 1)
                    for kt in range(KT):
                        last = nc.tensor.matmul(down_ps[:, 0:EXPERTS + ER], h_t[:, kt], down[:, kt], start=kt == 0, stop=kt == KT - 1)
                    last.then_inc(down_ready, 1)

            steps(pe, step)


def build_program(nc, io, out):
    io = dict(io, out=out)
    S = {
        "gates": nc.dram_tensor("gate_rows", [2, D], F32, kind="Internal").ap(),
        "q": nc.dram_tensor("q_split", [2, 2, HEADS, HALF, T], F32, kind="Internal").ap(),
        "k": nc.dram_tensor("k_split", [2, 2, KVH, HALF, T], F32, kind="Internal").ap(),
        "o": nc.dram_tensor("attention_split", [2, KVH, P, T], F32, kind="Internal").ap(),
    }
    ctx = ExitStack()
    with ctx:
        def sb(name, shape, dt=F32):
            return ctx.enter_context(nc.sbuf_tensor(name, shape, dt))

        M = {
            "ident": sb("identity", [P, P]),
            "ranks": sb("expert_ranks", [P, EXPERTS]),
            "masks": sb("masks_bf16", [P, 3, P], BF16),
            "mod": sb("modulation", [P, 4, KT]),
            "psum": ctx.enter_context(nc.psum_tensor("psum_banks", [P, 8, CH], F32)),
        }
        with ExitStack() as upto_attend:
            M["v_all"] = upto_attend.enter_context(nc.sbuf_tensor("v_all", [P, NTT, KV_W], F32))
            with ExitStack() as upto_project:
                M["w_hi"] = upto_project.enter_context(nc.sbuf_tensor("w_hi", [P, KT, WCOLS], F32R))
                M["w_lo"] = upto_project.enter_context(nc.sbuf_tensor("w_lo", [P, KT, WCOLS], F32R))
                modulate_block(nc, io, S, M)
                project_block(nc, io, S, M)
            attend_block(nc, io, S, M)
        feed_block(nc, io, S, M)


def shape_constants():
    base = np.float32(500000.0)
    exponent = np.arange(0, HD, 2, dtype=np.float32) / np.float32(HD)
    inv_freq = np.float32(1.0) / np.power(np.float64(base), exponent.astype(np.float64)).astype(np.float32)
    angle = np.arange(T, dtype=np.float32)[None, :] * inv_freq[:, None]
    trig = np.stack([np.cos(angle), np.sin(angle)], axis=1).astype(np.float32)
    trig = np.ascontiguousarray(np.tile(trig, (P // HALF, 1, 1)))
    consts = np.zeros((P, P + EXPERTS), np.float32)
    consts[:, :P] = np.eye(P)
    consts[:, P:] = EXPERTS - np.arange(EXPERTS)
    row, col = np.arange(P)[:, None], np.arange(P)[None, :]
    masks = np.stack([np.eye(P), np.where(col > row, MASKED, 0.0), np.where(row > col, MASKED, 0.0)], axis=1)
    return trig, consts, masks.astype(mybir.dt.np(BF16))


def kernel(**inputs):
    import concourse.bacc as bacc
    from concourse.bass_utils import run_bass_kernel_spmd

    a = {k: np.asarray(v) for k, v in inputs.items()}
    trig, consts, masks = shape_constants()
    wq = a["L0_attn_Wq"].reshape(D, QUNITS, HPU, 2, HALF).transpose(0, 1, 3, 2, 4).reshape(D, HEADS * HD)
    wk = a["L0_attn_Wk"].reshape(D, KVH, 2, HALF).transpose(0, 2, 1, 3).reshape(D, KV_W)
    arrays = {
        "x": a["L0_attn_x"].reshape(T, D),
        "wqkv": np.concatenate([wk, a["L0_attn_Wv"], wq], axis=1),
        "wo": a["L0_attn_Wo"],
        "down": np.concatenate([a["L0_ffn_route_w"], a["L0_ffn_A"].reshape(ER, D)], axis=0).T,
        "up": a["L0_ffn_Bw"].transpose(0, 2, 1).reshape(ER, D),
        "c": a["L0_c"],
        "wmod": a["L0_wmod"],
        "trig": trig,
        "consts": consts,
        "masks": masks,
    }
    nc = bacc.Bacc("TRN2", target_bir_lowering=False, num_devices=1)
    feeds, io = {}, {}
    for name, array in arrays.items():
        array = np.ascontiguousarray(array)
        feeds[f"in_{name}"] = array
        io[name] = nc.dram_tensor(f"in_{name}", array.shape, mybir.dt.from_np(array.dtype), kind="ExternalInput").ap()
    out = nc.dram_tensor("out_x", (T, D), F32, kind="ExternalOutput").ap()
    build_program(nc, io, out)
    result = run_bass_kernel_spmd(nc, [feeds], core_ids=[0])
    return result.results[0]["out_x"].reshape(1, T, D)
```

```python
from contextlib import ExitStack

import numpy as np

import concourse.bass as bass
from concourse import mybir

F32 = mybir.dt.float32
F32R = mybir.dt.float32r
BF16 = mybir.dt.bfloat16
ALU = mybir.AluOpType
ACT = mybir.ActivationFunctionType
AX = mybir.AxisListType

P = 128
T, D = 2048, 1024
HEADS, KVH, HD = 32, 8, 32
GRP = HEADS // KVH
HALF = HD // 2
KT = D // P
CH = 512
NCH = T // CH
TPC = CH // P
NTT = T // P
EXPERTS, RANK = 8, 16
ER = EXPERTS * RANK
LN_EPS = 1e-5
SCORE_SCALE = float(HD) ** -0.5
MASKED = -1e30

KV_W = KVH * HD
COL_K, COL_V, COL_Q = 0, KV_W, 2 * KV_W
WCOLS = COL_Q + HEADS * HD
HPU = P // HALF
QUNITS = HEADS // HPU
UNITS = 2 + QUNITS
ROPES = 1 + QUNITS

MODC = 256
MPP = D // MODC
MOD_RING = 4
SIDE = 4


def wait_past(eng, sem, value):
    if not isinstance(value, int) or value > 0:
        eng.wait_ge(sem, value)


def multiply_piece(nc, rows_ps, piece, c_act):
    for kk in range(KT):
        at = kk % SIDE * HD
        last = nc.tensor.matmul(rows_ps[at:at + HD], c_act[:, kk], piece[:, kk], start=kk < SIDE, stop=kk >= KT - SIDE)
    return last


def turn_piece(nc, cols_ps, rows, pick, at):
    for half in range(MODC // P):
        last = nc.tensor.matmul(cols_ps[:, at + half:at + half + 1], rows[:, half * P:(half + 1) * P], pick[:], start=True, stop=True)
    return last


def modulate_block(nc, io, S, M):
    ctx = ExitStack()
    with ctx:
        def sb(name, shape, dt=F32):
            return ctx.enter_context(nc.sbuf_tensor(name, shape, dt))

        def sem(name):
            return ctx.enter_context(nc.semaphore(name))

        c_col = sb("c_col", [P, KT])
        c_exp = sb("c_exp", [P, KT])
        c_den = sb("c_den", [P, KT])
        c_rec = sb("c_rec", [P, KT])
        piece = sb("wmod_piece", [P, MOD_RING, KT, MODC])
        wraw = sb("w_raw", [P, 2, WCOLS])
        rows = sb("mod_rows", [P, 2, MODC])
        cols_ps = M["psum"][:, 0, :]
        rows_ps = M["psum"][:, 1:3, 0:MODC]
        PIECES = 2 * MPP
        assert PIECES == KT

        c_in = sem("c_in")
        const_in = sem("const_in")
        piece_in = [sem(f"piece_in{i}") for i in range(MOD_RING)]
        piece_used = sem("piece_used")
        w_in = [sem(f"w_in{i}") for i in range(2)]
        w_hi_done = sem("w_hi_done")
        w_split = sem("w_split")
        exp_ready = sem("exp_ready")
        act_ready = sem("c_act_ready")
        chain = sem("mod_chain")
        pick_ready = sem("pick_ready")
        rows_copied = sem("rows_copied")
        turned = sem("rows_turned")
        block = ctx.enter_context(nc.Block())

        @block.sync
        def _(sp):
            sp.dma_start(c_col[:], io["c"].rearrange("a (p kk) -> (a p) kk", kk=KT)).then_inc(c_in, 16)
            sp.dma_start(M["ident"][:], io["consts"][:, 0:P]).then_inc(const_in, 16)
            sp.dma_start(M["ranks"][:], io["consts"][:, P:P + EXPERTS]).then_inc(const_in, 16)
            sp.dma_start(M["masks"][:], io["masks"]).then_inc(const_in, 16)
            wmod_v = io["wmod"].rearrange("(p kk) n -> p kk n", kk=KT)
            for n in range(PIECES):
                wait_past(sp, piece_used, n - MOD_RING + 1)
                sp.dma_start(piece[:, n % MOD_RING], wmod_v[:, :, n * MODC:(n + 1) * MODC]).then_inc(piece_in[n % MOD_RING], 16)
            for j in range(TPC):
                sp.dma_start(M["x"][:, j], io["x"][j * P:(j + 1) * P, :]).then_inc(M["x_in"][j], 16)

        @block.scalar
        def _(act):
            def load(kt):
                wait_past(act, w_split, kt - 1)
                act.dma_start(wraw[:, kt % 2], io["wqkv"][kt * P:(kt + 1) * P, :]).then_inc(w_in[kt % 2], 16)

            load(0)
            load(1)
            act.wait_ge(c_in, 16)
            nc.scalar.activation(c_exp[:], c_col[:], ACT.Exp, scale=-1.0).then_inc(exp_ready, 1)
            for kt in range(KT):
                act.wait_ge(w_in[kt % 2], 16 * (kt // 2 + 1))
                nc.scalar.activation(M["w_hi"][:, kt], wraw[:, kt % 2], ACT.Copy).then_inc(w_hi_done, 1)
                if kt + 2 < KT:
                    load(kt + 2)

        @block.vector
        def _(dve):
            done = 0

            def link(ins):
                nonlocal done
                done += 1
                ins.then_inc(chain, 1)
                dve.wait_ge(chain, done)

            dve.wait_ge(exp_ready, 1)
            link(nc.vector.tensor_scalar_add(c_den[:], c_exp[:], 1.0))
            link(nc.vector.reciprocal(c_rec[:], c_den[:]))
            def wide(col):
                return col[:].rearrange("p (k a) -> p k a", a=1).broadcast_to((P, KT, HD))

            nc.vector.tensor_tensor(M["c_act"][:], wide(c_col), wide(c_rec), ALU.mult).then_inc(act_ready, 1)
            dve.wait_ge(const_in, 48)
            nc.vector.tensor_reduce(M["pick"][:], M["ident"][:, 0:P:HD], op=ALU.add, axis=AX.X).then_inc(pick_ready, 1)
            for kt in range(KT):
                dve.wait_ge(w_hi_done, kt + 1)
                nc.vector.tensor_tensor(M["w_lo"][:, kt], wraw[:, kt % 2], M["w_hi"][:, kt].bitcast(F32),
                                        ALU.subtract).then_inc(w_split, 1)
                dve.wait_ge(piece_used, kt + 1)
                wait_past(dve, turned, kt - 1)
                nc.vector.tensor_copy(rows[:, kt % 2], rows_ps[:, kt % 2]).then_inc(rows_copied, 1)
            dve.wait_ge(turned, PIECES)
            nc.vector.tensor_copy(M["mod"][:, 0, :], cols_ps[:, 0:KT])
            nc.vector.tensor_scalar_add(M["mod"][:, 1, :], cols_ps[:, KT:2 * KT], 1.0)

        @block.tensor
        def _(pe):
            pe.wait_ge(act_ready, 1)
            for n in range(PIECES):
                pe.wait_ge(piece_in[n % MOD_RING], 16 * (n // MOD_RING + 1))
                wait_past(pe, rows_copied, n - 1)
                multiply_piece(nc, rows_ps[:, n % 2], piece[:, n % MOD_RING], M["c_act"]).then_inc(piece_used, 1)
                if n == 0:
                    pe.wait_ge(pick_ready, 1)
                else:
                    pe.wait_ge(rows_copied, n)
                    turn_piece(nc, cols_ps, rows[:, (n - 1) % 2], M["pick"], (n - 1) * (MODC // P)).then_inc(turned, 1)
            pe.wait_ge(rows_copied, PIECES)
            turn_piece(nc, cols_ps, rows[:, (PIECES - 1) % 2], M["pick"], (PIECES - 1) * (MODC // P)).then_inc(turned, 1)


def project_block(nc, io, S, M):
    ctx = ExitStack()
    with ctx:
        def sb(name, shape, dt=F32):
            return ctx.enter_context(nc.sbuf_tensor(name, shape, dt))

        def sem(name):
            return ctx.enter_context(nc.semaphore(name))

        x = M["x"]
        xn = sb("x_normed", [P, TPC, D])
        hf = sb("h_full", [P, 2, CH])
        h_hi = sb("h_hi", [P, KT, CH], F32R)
        h_lo = sb("h_lo", [P, KT, CH], F32R)
        trig = sb("trig", [P, 2, CH])
        by_cos = sb("by_cos", [P, 2, CH])
        by_sin = sb("by_sin", [P, 2, CH])
        rot = sb("rotated", [P, 2, CH])
        rot_hi = sb("rotated_hi", [P, 2, CH], F32R)
        rot_lo = sb("rotated_lo", [P, 2, CH], F32R)
        stats = sb("ln_stats", [P, TPC, 2, 6])
        meanvar = sb("ln_meanvar", [P, TPC, 2])
        var = sb("ln_var", [P, TPC])
        std = sb("ln_std", [P, TPC])
        cell = sb("hold_cell", [P, 1])
        r0 = sb("ln_r0", [P, TPC])
        r1 = sb("ln_r1", [P, TPC])
        r2 = sb("ln_r2", [P, TPC])
        rstd = sb("ln_rstd", [P, TPC])
        w_hi, w_lo, ident, mod, v_all = M["w_hi"], M["w_lo"], M["ident"], M["mod"], M["v_all"]
        unit_ps = M["psum"][:, 0:4].rearrange("p (s b) n -> p s b n", s=2)
        tr_ps = M["psum"][:, 4:8]

        x_in = M["x_in"]
        trig_in = sem("trig_in")
        var_ready = sem("var_ready")
        std_ready = sem("std_ready")
        xn_ready = sem("xn_ready")
        tr_ready = sem("tr_ready")
        hf_ready = sem("hf_ready")
        hh_ready = sem("hh_ready")
        h_ready = sem("h_ready")
        unit_ready = sem("unit_ready")
        v_read = sem("v_read")
        rope_read = sem("rope_read")
        rot_ready = sem("rot_ready")
        hi_ready = sem("hi_ready")
        lo_ready = sem("lo_ready")
        hi_out = sem("hi_out")
        lo_out = sem("lo_out")
        chain = sem("proj_chain")
        block = ctx.enter_context(nc.Block())

        q_dram, k_dram = S["q"], S["k"]

        @block.sync
        def _(sp):
            def load_x(n, j):
                sp.dma_start(x[:, j], io["x"][bass.ds(n * CH + j * P, P), :]).then_inc(x_in[j], 16)

            def chunk(n, first, last):
                if not first:
                    sp.wait_ge(rope_read, n * ROPES)
                sp.dma_start(trig[:], io["trig"][:, :, bass.ds(n * CH, CH)]).then_inc(trig_in, 16)
                if not last:
                    for j in range(TPC):
                        sp.wait_ge(xn_ready, n * TPC + j + 1)
                        load_x(n + 1, j)
                for r in range(ROPES):
                    for part, tile, ready, out in ((0, rot_hi, hi_ready, hi_out), (1, rot_lo, lo_ready, lo_out)):
                        sp.wait_ge(ready, n * ROPES + r + 1)
                        for b in range(2):
                            heads = slice(0, KVH) if r == 0 else slice((r - 1) * HPU, r * HPU)
                            dst = (k_dram if r == 0 else q_dram)[part, b, heads, :, bass.ds(n * CH, CH)]
                            sp.dma_start(dst.rearrange("h i t -> (h i) t"), tile[:, b].bitcast(F32)).then_inc(out, 16)

            chunk(0, True, False)
            with sp.Fori(1, NCH - 1) as n:
                chunk(n, False, False)
            chunk(NCH - 1, False, True)
            sp.wait_ge(hi_out, NCH * ROPES * 32)
            sp.wait_ge(lo_out, NCH * ROPES * 32)

        @block.scalar
        def _(act):
            def sqrt_of_var(n):
                act.wait_ge(var_ready, n + 1)
                nc.scalar.activation(std[:], var[:], ACT.Sqrt).then_inc(std_ready, 1)

            def rope_hi(n, r, first):
                act.wait_ge(rot_ready, n * ROPES + r + 1)
                if not (first and r == 0):
                    act.wait_ge(hi_out, (n * ROPES + r) * 32)
                nc.scalar.activation(rot_hi[:], rot[:], ACT.Copy).then_inc(hi_ready, 1)

            def chunk(n, first, last):
                for kt in range(KT):
                    act.wait_ge(tr_ready, n * KT + kt + 1)
                    if not (first and kt < 2):
                        act.wait_ge(h_ready, n * KT + kt - 1)
                    nc.scalar.activation(hf[:, kt % 2], tr_ps[:, kt % 4], ACT.Identity, bias=mod[:, 0, kt:kt + 1],
                                         scale=mod[:, 1, kt:kt + 1]).then_inc(hf_ready, 1)
                if not last:
                    sqrt_of_var(n + 1)
                rope_hi(n, 0, first)
                act.wait_ge(unit_ready, n * UNITS + 2)
                nc.scalar.activation(v_all[:, bass.ds(n * TPC, TPC), :], unit_ps[:, 1].rearrange("p b (j c) -> p (b j) c", j=2),
                                     ACT.Copy).then_inc(v_read, 1)
                for r in range(1, ROPES):
                    rope_hi(n, r, first)

            sqrt_of_var(0)
            chunk(0, True, False)
            with act.Fori(1, NCH - 1) as n:
                chunk(n, False, False)
            chunk(NCH - 1, False, True)

        @block.vector
        def _(dve):
            LINKS = TPC * 3 + 6

            def norm(n, first):
                base = n * LINKS
                k = 0

                def link(ins):
                    nonlocal k
                    k += 1
                    ins.then_inc(chain, 1)

                for j in range(TPC):
                    dve.wait_ge(x_in[j], (n + 1) * 16)
                    for half in range(2):
                        link(nc.vector.bn_stats(stats[:, j, half], x[:, j, half * CH:(half + 1) * CH]))
                dve.wait_ge(chain, base + k)
                link(nc.vector.tensor_copy(cell[:], ident[:, 0:1]))
                for j in range(TPC):
                    link(nc.vector.bn_aggr(meanvar[:, j], stats[:, j]))
                dve.wait_ge(chain, base + k)
                nc.vector.tensor_scalar_add(var[:], meanvar[:, :, 1], LN_EPS).then_inc(var_ready, 1)
                dve.wait_ge(std_ready, n + 1)
                link(nc.vector.reciprocal(r0[:], std[:]))
                dve.wait_ge(chain, base + k)
                link(nc.vector.tensor_tensor(r1[:], r0[:], r0[:], ALU.mult))
                dve.wait_ge(chain, base + k)
                link(nc.vector.tensor_tensor(r2[:], r1[:], var[:], ALU.mult))
                dve.wait_ge(chain, base + k)
                link(nc.vector.tensor_scalar(r1[:], r2[:], -0.5, 1.5, ALU.mult, ALU.add))
                dve.wait_ge(chain, base + k)
                link(nc.vector.tensor_tensor(rstd[:], r0[:], r1[:], ALU.mult))
                dve.wait_ge(chain, base + k)
                assert k == LINKS
                if not first:
                    dve.wait_ge(tr_ready, n * KT)
                for j in range(TPC):
                    nc.vector.tensor_scalar(xn[:, j], x[:, j], meanvar[:, j, 0:1], rstd[:, j:j + 1],
                                            ALU.subtract, ALU.mult).then_inc(xn_ready, 1)

            def split_lo(n, r, first):
                dve.wait_ge(hi_ready, n * ROPES + r + 1)
                if not (first and r == 0):
                    dve.wait_ge(lo_out, (n * ROPES + r) * 32)
                nc.vector.tensor_tensor(rot_lo[:], rot[:], rot_hi[:].bitcast(F32), ALU.subtract).then_inc(lo_ready, 1)

            def chunk(n, first, last):
                for kt in range(KT):
                    dve.wait_ge(hf_ready, n * KT + kt + 1)
                    if not first and kt == 0:
                        dve.wait_ge(unit_ready, n * UNITS)
                    nc.vector.tensor_copy(h_hi[:, kt], hf[:, kt % 2]).then_inc(hh_ready, 1)
                    dve.wait_ge(hh_ready, n * KT + kt + 1)
                    nc.vector.tensor_tensor(h_lo[:, kt], hf[:, kt % 2], h_hi[:, kt].bitcast(F32),
                                            ALU.subtract).then_inc(h_ready, 1)
                if not last:
                    norm(n + 1, False)
                dve.wait_ge(trig_in, (n + 1) * 16)
                for r in range(ROPES):
                    unit = 0 if r == 0 else r + 1
                    dve.wait_ge(unit_ready, n * UNITS + unit + 1)
                    if not (first and r == 0):
                        dve.wait_ge(rot_ready, n * ROPES + r)
                    for tile, f in ((by_cos, 0), (by_sin, 1)):
                        table = trig[:, f:f + 1, :].broadcast_to((P, 2, CH))
                        last_ins = nc.vector.tensor_tensor(tile[:], unit_ps[:, unit % 2], table, ALU.mult)
                    last_ins.then_inc(rope_read, 1)
                    if r:
                        split_lo(n, r - 1, first)
                split_lo(n, ROPES - 1, False)

            norm(0, True)
            chunk(0, True, False)
            with dve.Fori(1, NCH - 1) as n:
                chunk(n, False, False)
            chunk(NCH - 1, False, True)

        @block.gpsimd
        def _(pool):
            def chunk(n, first):
                for r in range(ROPES):
                    pool.wait_ge(rope_read, n * ROPES + r + 1)
                    if not (first and r == 0):
                        pool.wait_ge(lo_ready, n * ROPES + r)
                    nc.gpsimd.tensor_tensor(rot[:, 0], by_cos[:, 0], by_sin[:, 1], ALU.subtract)
                    nc.gpsimd.tensor_tensor(rot[:, 1], by_sin[:, 0], by_cos[:, 1], ALU.add).then_inc(rot_ready, 1)

            chunk(0, True)
            with pool.Fori(1, NCH) as n:
                chunk(n, False)

        @block.tensor
        def _(pe):
            def products(out, terms, start, stop):
                for i, (lhs, rhs) in enumerate(terms):
                    last = nc.tensor.matmul(out, lhs, rhs, start=start and i == 0, stop=stop and i == len(terms) - 1)
                return last

            def chunk(n, first):
                pe.wait_ge(xn_ready, (n + 1) * TPC)
                for kt in range(KT):
                    if not (first and kt < 4):
                        pe.wait_ge(hf_ready, n * KT + kt - 3)
                    for j in range(TPC):
                        last = nc.tensor.transpose(tr_ps[:, kt % 4, j * P:(j + 1) * P], xn[:, j, kt * P:(kt + 1) * P], ident[:])
                    last.then_inc(tr_ready, 1)
                for unit in range(UNITS):
                    if unit == 3:
                        pe.wait_ge(v_read, n + 1)
                    elif not (first and unit < 2):
                        pe.wait_ge(rope_read, n * ROPES + {0: -1, 1: 0, 2: 1, 4: 2, 5: 3}[unit])
                    if unit == 1:
                        for j in range(TPC):
                            out = unit_ps[:, 1, j // 2, (j % 2) * KV_W:(j % 2 + 1) * KV_W]
                            rows, cols = slice(j * P, (j + 1) * P), slice(COL_V, COL_V + KV_W)
                            for kt in range(KT):
                                last = products(out, ((h_hi[:, kt, rows], w_hi[:, kt, cols]), (h_hi[:, kt, rows], w_lo[:, kt, cols]),
                                                      (h_lo[:, kt, rows], w_hi[:, kt, cols])), kt == 0, kt == KT - 1)
                    else:
                        at = COL_K if unit == 0 else COL_Q + (unit - 2) * 2 * P
                        for kt in range(KT):
                            if unit == 0:
                                pe.wait_ge(h_ready, n * KT + kt + 1)
                            for b in range(2):
                                cols = slice(at + b * P, at + (b + 1) * P)
                                last = products(unit_ps[:, unit % 2, b], ((w_hi[:, kt, cols], h_hi[:, kt]), (w_hi[:, kt, cols], h_lo[:, kt]),
                                                                          (w_lo[:, kt, cols], h_hi[:, kt])), kt == 0, kt == KT - 1)
                    last.then_inc(unit_ready, 1)

            chunk(0, True)
            with pe.Fori(1, NCH) as n:
                chunk(n, False)


def attend_block(nc, io, S, M):
    ctx = ExitStack()
    with ctx:
        def sb(name, shape, dt=F32):
            return ctx.enter_context(nc.sbuf_tensor(name, shape, dt))

        def sem(name):
            return ctx.enter_context(nc.semaphore(name))

        piece_place = ExitStack()
        piece = piece_place.enter_context(nc.sbuf_tensor("wmod_piece2", [P, MOD_RING, KT, MODC], F32))
        piece_place.close()
        NP = 8
        probs = sb("probs", [P, NP, GRP, CH])
        gate_col = sb("gate_col", [P, 2, KT])
        gate_neg = sb("gate_neg", [P, 2, KT])
        gate_abs = sb("gate_abs", [P, 2, KT])
        gate_sgn = sb("gate_sgn", [P, 2, KT])
        gate_fin = sb("gate_fin", [P, 2, KT])
        gate_row = sb("gate_row", [2 * KT, P])
        mod_rows = sb("mod_rows2", [P, 2, MODC])
        PIECES = range(2 * MPP, 6 * MPP)
        GA_AT, SB_AT, CB_AT, GB_AT = 0, KT, 2 * KT, 3 * KT
        ONES_ROW = 3 * HD
        qs = [sb(f"q_stack{u}", [ONES_ROW + 1, NCH, GRP, CH], F32R) for u in range(2)]
        ks = [sb(f"k_stack{u}", [ONES_ROW + 1, T], F32R) for u in range(2)]
        v_g = [sb(f"v_group{u}", [P, NTT, HD]) for u in range(2)]
        sums = sb("prob_sums", [P, 2, GRP, CH])
        part_max = sb("part_max", [P, NTT, NCH + 1, GRP])
        HEAD, TAIL = 0, 1
        CHUNKS_OF = [range(NCH - 1), range(NCH - 1, NCH)]
        q_max = sb("q_max", [P, 2, P])
        neg_max = [sb(f"neg_max{part}", [len(CHUNKS_OF[part]) * GRP * TPC, P], F32R) for part in range(2)]
        ones = sb("ones_sum", [P, HD])
        o_raw = sb("o_raw", [P, CH])
        o_sum = sb("o_sum", [P, CH])
        o_rec = sb("o_rec", [P, CH])
        o_full = sb("o_full", [P, CH])
        o_hi = sb("o_hi", [P, CH], F32R)
        o_lo = sb("o_lo", [P, CH], F32R)
        ident, masks, v_all = M["ident"], M["masks"], M["v_all"]
        ident_b, mask_qk, mask_kq = masks[:, 0], masks[:, 1], masks[:, 2]

        def four(mask):
            return mask.rearrange("p (a t) -> p a t", a=1).broadcast_to((P, GRP, P))

        max_ps = M["psum"][:, 0:4].rearrange("p (s b) n -> p s b n", s=2)
        score_ps = M["psum"][:, 4:6]
        out_ps = M["psum"][:, 6]
        sum_ps = M["psum"][:, 7]
        rows_ps = M["psum"][:, 6:8, 0:MODC]

        STEPS = [(c, kb) for c in range(NCH) for kb in range((c + 1) * TPC)]
        LAST = [max(n for n, st in enumerate(STEPS) if st[0] == c) for c in range(NCH)]
        NS = len(STEPS)

        def score_units(n):
            c, kb = STEPS[n]
            if kb < c * TPC:
                return [((j, j + 1), (0, CH), False) for j in range(GRP)]
            off = kb * P - c * CH
            out, rest = [((0, GRP), (off, off + P), True)], CH - off - P
            if rest:
                k = min(GRP, CH // rest)
                k = {1: 1, 2: 2, 4: 4}[k]
                out += [((j, j + k), (off + P, CH), False) for j in range(0, GRP, k)]
            return out

        UNITS_OF = [score_units(n) for n in range(NS)]
        BEFORE = [sum(len(u) for u in UNITS_OF[:n]) for n in range(NS + 1)]
        NU = BEFORE[NS]
        assert NU % 2 == 0 and NS % NP == 0

        ADDED = [[], [0, 1, 2, 3], [0, 1, 2, 4, 6, 7, 8], [0, 1, 2, 4, 6, 7, 9, 11, 12]]
        ADDS = [max(0, len(a) - 1) for a in ADDED]
        NADD = sum(ADDS)

        def add_after(c, kb):
            return sum(ADDS[:c]) + max(1, ADDED[c].index(kb))

        def max_units():
            out = []
            for qb in range(NTT):
                c, r = divmod(qb, TPC)
                for kc in range(c):
                    for hp in range(2):
                        out.append((qb, kc, [(b, 0, 2 * hp + b, kc * CH, CH) for b in range(2)], None, ("pair", hp, CH)))
                diag = [(0, j * P, j, qb * P, P) for j in range(GRP)]
                if r == 1:
                    out.append((qb, c, diag + [(1, j * P, j, c * CH, P) for j in range(GRP)], 0, ("both", 0, P)))
                    continue
                out.append((qb, c, diag, 0, ("diag", 0, P)))
                if r == 2:
                    out.append((qb, c + 1, [(j // 2, j % 2 * 2 * P, j, c * CH, 2 * P) for j in range(GRP)], None, ("four", 0, 2 * P)))
                if r == 3:
                    for hp in range(2):
                        out.append((qb, c + 1, [(b, 0, 2 * hp + b, c * CH, 3 * P) for b in range(2)], None, ("pair", hp, 3 * P)))
            return out

        MAXES = max_units()
        NM = len(MAXES)
        assert NM % 2 == 0 and NM // 2 > TPC
        NHEAD = min(m for m in range(NM) if MAXES[m][0] >= NTT - TPC)
        TURN = [-1, NM]
        TAIL_STEPS, HEAD_STEPS = (0, 20), (21, 37)
        COPY_V = 5
        LOADS = 12
        FIRST_PIECE = 6
        LAG = 2

        piece_in = [sem(f"piece2_in{i}") for i in range(MOD_RING)]
        piece_used = sem("piece2_used")
        rows_copied = sem("rows2_copied")
        rows_turned = sem("rows2_turned")
        mod_chain = sem("gate_chain")
        gate_ready = sem("gate_ready")
        gate_turned = sem("gate_turned")
        gate_out = sem("gate_out")
        load_in = [sem(f"load_in{u}") for u in range(2)]
        negmax_in = [sem(f"negmax_in{u}") for u in range(2)]
        ones_ready = sem("ones_ready")
        v_ready = sem("v_ready")
        score_ready = sem("score_ready")
        prob_ready = sem("prob_ready")
        step_done = sem("step_done")
        max_ready = sem("max_ready")
        max_read = sem("max_read")
        qmax_ready = sem("qmax_ready")
        maxt_ready = sem("maxt_ready")
        negmax_ready = sem("negmax_ready")
        sum_added = sem("sum_added")
        raw_ready = sem("raw_ready")
        rec_ready = sem("rec_ready")
        o_ready = sem("o_ready")
        hi_ready = sem("o_hi_ready")
        split_ready = sem("o_split_ready")
        o_out = sem("o_out")
        block = ctx.enter_context(nc.Block())

        def passes(eng, one):
            one(0, 0, False, True)
            one(0, 0, True, True)
            with eng.Fori(0, (KVH - 2) // 2) as i:
                one(i, 1, True, True)
                one(i + 1, 0, True, True)
            one(KVH // 2 - 1, 1, True, False)

        def unit_view(unit, heads, width):
            return score_ps[:, unit % 2, 0:heads * width].rearrange("p (j t) -> p j t", j=heads)

        def after(h, u, weigh):
            if not weigh:
                return h, u
            return (h, 1) if u == 0 else (h + 1, 0)

        def spread(units, steps, out):
            lo, hi = steps
            work = [GRP * (CH - max(0, kb * P - c * CH)) for c, kb in STEPS]
            size = [sum(p[4] for p in MAXES[m][2]) for m in units]
            seen, done, n = 0, work[lo], lo
            for m, part in zip(units, size):
                while seen * sum(work[lo:hi]) >= done * sum(size):
                    n += 1
                    done += work[n]
                out[n].append(m)
                seen += part

        def schedule(weigh, maxima):
            tail, head = [[] for _ in STEPS], [[] for _ in STEPS]
            if not weigh:
                return tail[:1], [[*range(NHEAD), TURN[HEAD]]]
            spread(range(NHEAD, NM), TAIL_STEPS, tail)
            tail[TAIL_STEPS[1]].append(TURN[TAIL])
            if maxima:
                spread(range(NHEAD), HEAD_STEPS, head)
                head[HEAD_STEPS[1]].append(TURN[HEAD])
            return tail, head

        @block.sync
        def _(sp):
            def store(s, c):
                sp.wait_ge(split_ready, s * NCH + c + 1)
                for part, tile in ((0, o_hi), (1, o_lo)):
                    sp.dma_start(S["o"][part, bass.ds(s, 1), :, c * CH:(c + 1) * CH].rearrange("a p t -> (a p) t"),
                                 tile[:].bitcast(F32)).then_inc(o_out, 16)

            def maxima_row(g, v, part):
                sp.wait_ge(negmax_ready, g * 2 + part + 1)
                chunks = CHUNKS_OF[part]
                sp.dma_start(qs[v][ONES_ROW:ONES_ROW + 1, chunks[0]:chunks[-1] + 1].bitcast(F32)
                             .rearrange("a c j (b t) -> a (c j b) t", t=P), neg_max[part][:].bitcast(F32)).then_inc(negmax_in[v], 16)

            def one(h, u, weigh, maxima):
                s = h * 2 + u
                gh, v = after(h, u, weigh)
                g = gh * 2 + v
                if maxima:
                    wait_past(sp, step_done, s * NS)
                    for block_of_rows, q_part, k_part in ((0, 0, 0), (1, 0, 1), (2, 1, 0)):
                        for b in range(2):
                            at = block_of_rows * HD + b * HALF
                            sp.dma_start(ks[v][at:at + HALF].bitcast(F32),
                                         S["k"][k_part, b, bass.ds(g, 1)].rearrange("a i t -> (a i) t")).then_inc(load_in[v], 16)
                            sp.dma_start(qs[v][at:at + HALF].bitcast(F32),
                                         S["q"][q_part, b, bass.ds(g * GRP, GRP)].rearrange("j i (c t) -> i c j t", t=CH)).then_inc(load_in[v], 16)
                if weigh:
                    if not isinstance(s, int) or s > 0:
                        store(s - 1, NCH - 1)
                    store(s, 0)
                    maxima_row(s, u, TAIL)
                    for c in range(1, NCH - 1):
                        store(s, c)
                if maxima:
                    maxima_row(g, v, HEAD)

            passes(sp, one)
            store(KVH - 1, NCH - 1)
            sp.wait_ge(o_out, KVH * NCH * 32)

        @block.scalar
        def _(act):
            def one(h, u, weigh, maxima):
                s = h * 2 + u

                def copy_out(c):
                    act.wait_ge(step_done, s * NS + LAST[c] + 1)
                    wait_past(act, o_ready, s * NCH + c)
                    nc.scalar.activation(o_sum[:], sum_ps, ACT.Copy)
                    nc.scalar.activation(o_raw[:], out_ps, ACT.Copy).then_inc(raw_ready, 1)

                if not weigh:
                    wmod_v = io["wmod"].rearrange("(p kk) n -> p kk n", kk=KT)

                    def load(i):
                        n = PIECES[i]
                        act.dma_start(piece[:, i % MOD_RING], wmod_v[:, :, n * MODC:(n + 1) * MODC]).then_inc(piece_in[i % MOD_RING], 16)

                    act.wait_ge(load_in[0], LOADS * 16)
                    for i in range(MOD_RING):
                        load(i)
                    for i in range(len(PIECES)):
                        act.wait_ge(piece_used, i + 1)
                        wait_past(act, rows_turned, i - 1)
                        nc.scalar.activation(mod_rows[:, i % 2], rows_ps[:, i % 2], ACT.Copy).then_inc(rows_copied, 1)
                        if i + MOD_RING < len(PIECES):
                            load(i + MOD_RING)
                    act.wait_ge(gate_turned, 2)
                    act.dma_start(S["gates"].rearrange("g (k p) -> (g k) p", p=P), gate_row[:]).then_inc(gate_out, 16)
                    act.wait_ge(gate_out, 16)
                    return
                for n in range(NS):
                    wait_past(act, step_done, s * NS + n - NP + 1)
                    old = (n - NP) % NS
                    oc, okb = STEPS[old]
                    if okb in ADDED[oc]:
                        group = s if n >= NP else s - 1
                        if not isinstance(group, int) or group >= 0:
                            act.wait_ge(sum_added, group * NADD + add_after(oc, okb))
                    for k, ((j0, j1), (c0, c1), _) in enumerate(UNITS_OF[n]):
                        unit = BEFORE[n] + k
                        act.wait_ge(score_ready, s * NU + unit + 1)
                        nc.scalar.activation(probs[:, n % NP, j0:j1, c0:c1], unit_view(unit, j1 - j0, c1 - c0), ACT.Exp,
                                             scale=SCORE_SCALE).then_inc(prob_ready, 1)
                        if k == min(1, len(UNITS_OF[n]) - 1) and n - LAG in LAST:
                            copy_out(STEPS[n - LAG][0])
                copy_out(NCH - 1)

            passes(act, one)

        @block.gpsimd
        def _(pool):
            nc.gpsimd.memset(ones[:], 1.0).then_inc(ones_ready, 1)
            nc.gpsimd.memset(q_max[:], 0.0).then_inc(ones_ready, 1)
            for c in range(NCH):
                nc.gpsimd.memset(part_max[:, c * TPC, c + 1], MASKED).then_inc(ones_ready, 1)
            for v in range(2):
                pool.wait_ge(ones_ready, v + 2 + NCH)
                nc.gpsimd.memset(ks[v][ONES_ROW:ONES_ROW + 1].bitcast(F32), 1.0).then_inc(ones_ready, 1)

            def one(h, u, weigh, maxima):
                s = h * 2 + u
                if not weigh:
                    return
                def split(c, s):
                    pool.wait_ge(hi_ready, s * NCH + c + 1)
                    wait_past(pool, o_out, (s * NCH + c) * 32)
                    nc.gpsimd.tensor_tensor(o_lo[:], o_full[:], o_hi[:].bitcast(F32), ALU.subtract).then_inc(split_ready, 1)

                if not isinstance(s, int) or s > 0:
                    split(NCH - 1, s - 1)
                for c in range(1, NCH):
                    total = sums[:, (c - 1) % 2]
                    for i, kb in enumerate(ADDED[c][1:]):
                        n = STEPS.index((c, kb))
                        if i == 0 and c != NCH - 1:
                            wait_past(pool, step_done, (s - 1) * NS + LAST[NCH - 1] + 1 if c == 1 else 0)
                        elif i == 0:
                            pool.wait_ge(step_done, s * NS + LAST[1] + 1)
                        pool.wait_ge(prob_ready, s * NU + BEFORE[n + 1])
                        if i:
                            pool.wait_ge(sum_added, s * NADD + sum(ADDS[:c]) + i)
                        first = probs[:, STEPS.index((c, ADDED[c][0])) % NP] if i == 0 else total
                        nc.gpsimd.tensor_tensor(total, first, probs[:, n % NP], ALU.add).then_inc(sum_added, 1)
                        if i == min(3, ADDS[c] - 1):
                            split(c - 1, s)

            passes(pool, one)
            pool.wait_ge(hi_ready, KVH * NCH)
            pool.wait_ge(o_out, (KVH * NCH - 1) * 32)
            nc.gpsimd.tensor_tensor(o_lo[:], o_full[:], o_hi[:].bitcast(F32), ALU.subtract).then_inc(split_ready, 1)

        @block.vector
        def _(dve):
            dve.wait_ge(ones_ready, 4 + NCH)

            def modulation():
                cols, mod, done = score_ps[:, 0], M["mod"], 0

                def link(ins):
                    nonlocal done
                    done += 1
                    ins.then_inc(mod_chain, 1)
                    dve.wait_ge(mod_chain, done)

                dve.wait_ge(rows_turned, len(PIECES))
                nc.vector.tensor_copy(mod[:, 2, :], cols[:, SB_AT:SB_AT + KT])
                nc.vector.tensor_scalar_add(mod[:, 3, :], cols[:, CB_AT:CB_AT + KT], 1.0)
                nc.vector.tensor_copy(gate_col[:, 0], cols[:, GA_AT:GA_AT + KT])
                link(nc.vector.tensor_copy(gate_col[:, 1], cols[:, GB_AT:GB_AT + KT]))
                link(nc.vector.tensor_scalar(gate_neg[:], gate_col[:], -1.0, None, ALU.mult))
                link(nc.vector.tensor_tensor(gate_abs[:], gate_col[:], gate_neg[:], ALU.max))
                link(nc.vector.tensor_scalar(gate_sgn[:], gate_col[:], 0.0, 2.0, ALU.is_ge, ALU.mult))
                link(nc.vector.tensor_scalar(gate_neg[:], gate_sgn[:], 1.0, None, ALU.subtract))
                link(nc.vector.tensor_scalar(gate_sgn[:], gate_abs[:], 0.25, None, ALU.max))
                nc.vector.tensor_tensor(gate_fin[:], gate_sgn[:], gate_neg[:], ALU.mult).then_inc(gate_ready, 1)
                dve.wait_ge(gate_turned, 1)
                nc.vector.tensor_copy(gate_row[:], score_ps[0:2 * KT, 1, 0:P]).then_inc(gate_turned, 1)

            def one(h, u, weigh, maxima):
                s = h * 2 + u
                gh, v = after(h, u, weigh)
                g = gh * 2 + v
                tail, head = schedule(weigh, maxima)

                def values_of_group():
                    wait_past(dve, step_done, s * NS)
                    nc.vector.tensor_copy(v_g[v][:], v_all[:, :, bass.ds(g * HD, HD)]).then_inc(v_ready, 1)

                def negate(g, part, last_out):
                    dve.wait_ge(maxt_ready, g * 2 + part + 1)
                    wait_past(dve, *last_out)
                    rows = neg_max[part].shape[0]
                    nc.vector.tensor_scalar(neg_max[part][:], max_ps[0:rows, 0, 0, 0:P], -1.0, None,
                                            ALU.mult).then_inc(negmax_ready, 1)

                def take_max(g, m):
                    if m == TURN[HEAD]:
                        negate(g, HEAD, (negmax_in[1 - v], (gh + v - 1) * 32 + 16 if weigh else 0))
                        return
                    if m == TURN[TAIL]:
                        negate(g, TAIL, (negmax_in[1 - u], (h + u) * 32))
                        return
                    dve.wait_ge(max_ready, g * NM + m + 1)
                    qb, slot, _, _, (kind, hp, w) = MAXES[m]
                    banks = max_ps[:, m % 2]
                    if kind == "pair":
                        src, dst = banks[:, :, 0:w], part_max[:, qb, slot, 2 * hp:2 * hp + 2]
                    elif kind == "four":
                        src, dst = banks.rearrange("p b (j t) -> p (b j) t", t=w), part_max[:, qb, slot]
                    elif kind == "diag":
                        src, dst = banks[:, 0].rearrange("p (j t) -> p j t", t=w), part_max[:, qb, slot]
                    else:
                        src = banks.rearrange("p b (j t) -> p (b j) t", t=w)
                        dst = part_max[:, qb, slot:slot + 2].rearrange("p e j -> p (e j)")
                    nc.vector.tensor_reduce(dst, src, op=ALU.max, axis=AX.X).then_inc(max_read, 1)
                    if m in (NHEAD - 1, NM - 1):
                        part = HEAD if m == NHEAD - 1 else TAIL
                        dve.wait_ge(max_read, g * NM + m + 1)
                        for i, c in enumerate(CHUNKS_OF[part]):
                            tiles = slice(c * TPC, (c + 1) * TPC)
                            place = q_max[:, part, i * GRP * TPC:(i + 1) * GRP * TPC]
                            last = nc.vector.tensor_reduce(place.rearrange("p (j b) -> p b j", j=GRP),
                                                           part_max[:, tiles, 0:c + 2].rearrange("p b e j -> p b j e"),
                                                           op=ALU.max, axis=AX.X)
                        last.then_inc(qmax_ready, 1)

                def normalise(c, q):
                    cols = slice(q * P, (q + 1) * P)
                    if q == 0:
                        dve.wait_ge(raw_ready, s * NCH + c + 1)
                        wait_past(dve, split_ready, s * NCH + c)
                        wait_past(dve, o_out, (s * NCH + c) * 32)
                    nc.vector.reciprocal(o_rec[:, cols], o_sum[:, cols]).then_inc(rec_ready, 1)
                    dve.wait_ge(rec_ready, (s * NCH + c) * TPC + q + 1)
                    ins = nc.vector.tensor_tensor(o_full[:, cols], o_raw[:, cols], o_rec[:, cols], ALU.mult)
                    if q == TPC - 1:
                        ins.then_inc(o_ready, 1)
                        dve.wait_ge(o_ready, s * NCH + c + 1)
                        nc.vector.tensor_copy(o_hi[:], o_full[:]).then_inc(hi_ready, 1)

                if not weigh:
                    values_of_group()
                    for m in head[0]:
                        take_max(g, m)
                    modulation()
                    return
                for n in range(NS):
                    if n == COPY_V and maxima:
                        values_of_group()
                    for q in range(TPC):
                        if n - LAG - 1 - q in LAST:
                            normalise(STEPS[n - LAG - 1 - q][0], q)
                    for m in tail[n]:
                        take_max(s, m)
                    for m in head[n]:
                        take_max(g, m)
                for q in range(TPC):
                    normalise(NCH - 1, q)

            passes(dve, one)

        @block.tensor
        def _(pe):
            pe.wait_ge(ones_ready, 4 + NCH)

            def one(h, u, weigh, maxima):
                s = h * 2 + u
                gh, v = after(h, u, weigh)
                g = gh * 2 + v
                tail, head = schedule(weigh, maxima)

                def max_unit(g, gh, v, m):
                    if m in TURN:
                        part = TURN.index(m)
                        pe.wait_ge(qmax_ready, g * 2 + part + 1)
                        nc.tensor.transpose(max_ps[:, 0, 0, 0:P], q_max[:, part], ident[:]).then_inc(maxt_ready, 1)
                        return
                    if m == 0:
                        pe.wait_ge(load_in[v], (gh + 1) * LOADS * 16)
                        wait_past(pe, negmax_ready, g * 2)
                    if m == NHEAD + 1:
                        pe.wait_ge(negmax_ready, g * 2 + 1)
                    if m >= 2:
                        pe.wait_ge(max_read, g * NM + m - 1)
                    qb, _, pieces, diag, _ = MAXES[m]
                    for i, (b, at, j, k0, kn) in enumerate(pieces):
                        first = i == 0 or pieces[i - 1][0] != b
                        final = i == len(pieces) - 1 or pieces[i + 1][0] != b
                        last = nc.tensor.matmul(max_ps[:, m % 2, b, at:at + kn], qs[v][0:ONES_ROW, qb // TPC, j, qb % TPC * P:(qb % TPC + 1) * P],
                                                ks[v][0:ONES_ROW, k0:k0 + kn], start=first, stop=final and diag != b)
                        if final and diag == b:
                            last = nc.tensor.matmul(max_ps[:, m % 2, b].rearrange("p (j t) -> p j t", t=P), ident_b,
                                                    four(mask_qk), start=False, stop=True)
                    last.then_inc(max_ready, 1)

                if not weigh:
                    done = 0

                    def turn(i):
                        pe.wait_ge(rows_copied, i + 1)
                        turn_piece(nc, score_ps[:, 0], mod_rows[:, i % 2], M["pick"], i * (MODC // P)).then_inc(rows_turned, 1)

                    for m in head[0]:
                        max_unit(g, gh, v, m)
                        while done < len(PIECES) and (m - FIRST_PIECE + 1) * len(PIECES) >= (done + 1) * (NHEAD - 1 - FIRST_PIECE):
                            pe.wait_ge(piece_in[done % MOD_RING], 16 * (done // MOD_RING + 1))
                            wait_past(pe, rows_copied, done - 1)
                            multiply_piece(nc, rows_ps[:, done % 2], piece[:, done % MOD_RING], M["c_act"]).then_inc(piece_used, 1)
                            if done:
                                turn(done - 1)
                            done += 1
                    assert done == len(PIECES)
                    turn(len(PIECES) - 1)
                    pe.wait_ge(gate_ready, 1)
                    nc.tensor.transpose(score_ps[0:2 * KT, 1, 0:P], gate_fin[:].rearrange("p g k -> p (g k)"),
                                        ident[:]).then_inc(gate_turned, 1)
                    pe.wait_ge(gate_turned, 2)
                    return

                def scores(n, part):
                    c, kb = STEPS[n]
                    if n == LAST[NCH - 2] + 1 and part == 0:
                        pe.wait_ge(negmax_in[u], h * 32 + 32)
                    for k, ((j0, j1), (c0, c1), masked) in enumerate(UNITS_OF[n]):
                        if (k >= 2) != (part == 1):
                            continue
                        unit = BEFORE[n] + k
                        wait_past(pe, prob_ready, s * NU + unit - 1)
                        out = unit_view(unit, j1 - j0, c1 - c0)
                        last = nc.tensor.matmul(out, ks[u][:, kb * P:(kb + 1) * P], qs[u][:, c, j0:j1, c0:c1],
                                                start=True, stop=not masked)
                        if masked:
                            last = nc.tensor.matmul(out, ident_b, four(mask_kq), start=False, stop=True)
                        last.then_inc(score_ready, 1)

                def values(n):
                    c, kb = STEPS[n]
                    off = max(0, kb * P - c * CH)
                    if kb == 0:
                        wait_past(pe, raw_ready, s * NCH + c)
                    pe.wait_ge(prob_ready, s * NU + BEFORE[n + 1])
                    for j in range(GRP):
                        last = nc.tensor.matmul(out_ps[j * HD:(j + 1) * HD, off:], v_g[u][:, kb], probs[:, n % NP, j, off:],
                                                start=(kb == 0), stop=n in LAST)
                    summed = [] if kb in ADDED[c] else [(probs[:, n % NP], off)]
                    if n in LAST and ADDED[c]:
                        summed.append((sums[:, (c - 1) % 2], 0))
                    begin = kb == min(b for b in range(NTT) if b not in ADDED[c])
                    for i, (tile, at) in enumerate(summed):
                        if i == 1:
                            pe.wait_ge(sum_added, s * NADD + sum(ADDS[:c + 1]))
                        for j in range(GRP):
                            last = nc.tensor.matmul(sum_ps[j * HD:(j + 1) * HD, at:], ones[:], tile[:, j, at:], start=begin,
                                                    stop=n in LAST and i == len(summed) - 1)
                    last.then_inc(step_done, 1)

                pe.wait_ge(v_ready, s + 1)
                pe.wait_ge(negmax_in[u], h * 32 + 16)
                for n in range(NS + LAG):
                    if n < NS:
                        scores(n, 0)
                    if n >= LAG:
                        values(n - LAG)
                    if n < NS:
                        scores(n, 1)
                        for m in tail[n]:
                            max_unit(s, h, u, m)
                        for m in head[n]:
                            max_unit(g, gh, v, m)

            passes(pe, one)


def feed_block(nc, io, S, M):
    ctx = ExitStack()
    with ctx:
        def sb(name, shape, dt=F32):
            return ctx.enter_context(nc.sbuf_tensor(name, shape, dt))

        def sem(name):
            return ctx.enter_context(nc.semaphore(name))

        RING = 4
        wo_hi = sb("wo_hi", [P, KT, D], F32R)
        wo_lo = sb("wo_lo", [P, KT, D], F32R)
        wo_raw = sb("wo_raw", [P, 2, D])
        down = sb("router_and_a", [P, KT, EXPERTS + ER])
        up = sb("lora_b", [P, D])
        gates = sb("gates", [P, 2, D])
        o_hi = sb("att_hi", [P, 2, KVH, P], F32R)
        o_lo = sb("att_lo", [P, 2, KVH, P], F32R)
        x_t = sb("x_tile", [P, 2, D])
        gated = sb("gated", [P, D])
        x1 = sb("x_mid", [P, RING, D])
        xn = sb("x_mid_normed", [P, D])
        h_t = sb("h_transposed", [P, KT, P])
        cell = sb("hold_cell2", [P, 1])
        top = sb("top_logit", [P, 1])
        top_rank = sb("top_rank", [P, 1])
        rank = sb("rank_where_top", [P, EXPERTS])
        route = sb("route_weight", [P, EXPERTS])
        wh = sb("weighted_h", [P, ER])
        wh_t = sb("weighted_h_t", [P, P])
        lora = sb("lora_gated", [P, D])
        y = sb("y_tile", [P, 2, D])
        stats = sb("ln2_stats", [P, 2, 6])
        meanvar = sb("ln2_meanvar", [P, 2])
        var = sb("ln2_var", [P, 1])
        std = sb("ln2_std", [P, 1])
        r0 = sb("ln2_r0", [P, 1])
        r1 = sb("ln2_r1", [P, 1])
        r2 = sb("ln2_r2", [P, 1])
        rstd = sb("ln2_rstd", [P, 1])
        ident, mod, ranks = M["ident"], M["mod"], M["ranks"]
        proj_ps = M["psum"][:, 0:2]
        tr_ps = M["psum"][:, 2:4].rearrange("p b (k t) -> p (b k) t", t=P)
        down_ps = M["psum"][:, 4]
        wht_ps = M["psum"][:, 5, 0:P]
        up_ps = M["psum"][:, 6:8]

        wo_in = [sem(f"wo_in{i}") for i in range(2)]
        wo_hi_ready = sem("wo_hi_ready")
        wo_split = sem("wo_split")
        small_in = sem("small_in")
        o_in = [sem(f"att_in{i}") for i in range(2)]
        x_in = [sem(f"x_tile_in{i}") for i in range(2)]
        y_out = [sem(f"y_out{i}") for i in range(2)]
        proj_ready = sem("proj_ready")
        proj_read = sem("proj_read")
        x1_ready = sem("x1_ready")
        var_ready = sem("var2_ready")
        std_ready = sem("std2_ready")
        xn_ready = sem("xn2_ready")
        tr_ready = sem("tr2_ready")
        h_ready = sem("h2_ready")
        down_ready = sem("down_ready")
        wh_ready = sem("wh_ready")
        wht_ready = sem("wht_ready")
        wht_read = sem("wht_read")
        up_ready = sem("up_ready")
        up_read = sem("up_read")
        y_ready = sem("y_ready")
        chain0, chain1 = sem("norm_chain"), sem("route_chain")
        block = ctx.enter_context(nc.Block())

        def steps(eng, step):
            for t in range(RING):
                step(t, t, t // 2, True, t >= 1, t >= 2)
            with eng.Fori(1, NTT // RING) as i:
                for r in range(RING):
                    step(i * RING + r, r, i * (RING // 2) + r // 2, True, True, True)
            step(NTT, 0, NTT // 2, False, True, True)
            step(NTT + 1, 1, NTT // 2, False, False, True)

        @block.sync
        def _(sp):
            def step(t, r, pairs, has0, has1, has2):
                if has0:
                    wait_past(sp, proj_ready, (t - 1) * 2)
                    for part, tile in ((0, o_hi), (1, o_lo)):
                        sp.dma_start(tile[:, r % 2].bitcast(F32), S["o"][part, :, :, bass.ds(t * P, P)].rearrange("g p t -> p g t"))\
                          .then_inc(o_in[r % 2], 16)
                    wait_past(sp, x1_ready, (t - 1) * 2)
                    sp.dma_start(x_t[:, r % 2], io["x"][bass.ds(t * P, P), :]).then_inc(x_in[r % 2], 16)
                if has2:
                    sp.wait_ge(y_ready, t - 1)
                    sp.dma_start(io["out"][bass.ds((t - 2) * P, P), :], y[:, r % 2]).then_inc(y_out[r % 2], 16)

            steps(sp, step)
            for i in range(2):
                sp.wait_ge(y_out[i], NTT // 2 * 16)

        @block.scalar
        def _(act):
            act.dma_start(gates[:], S["gates"].partition_broadcast(P)).then_inc(small_in, 16)
            act.dma_start(down[:], io["down"].rearrange("(k p) n -> p k n", p=P)).then_inc(small_in, 16)
            act.dma_start(up[:], io["up"]).then_inc(small_in, 16)

            def load(kt):
                wait_past(act, wo_split, kt - 1)
                act.dma_start(wo_raw[:, kt % 2], io["wo"][kt * P:(kt + 1) * P, :]).then_inc(wo_in[kt % 2], 16)

            load(0)
            load(1)
            for kt in range(KT):
                act.wait_ge(wo_in[kt % 2], 16 * (kt // 2 + 1))
                nc.scalar.activation(wo_hi[:, kt], wo_raw[:, kt % 2], ACT.Copy).then_inc(wo_hi_ready, 1)
                if kt + 2 < KT:
                    load(kt + 2)

            def step(t, r, pairs, has0, has1, has2):
                if has2:
                    act.wait_ge(wht_ready, t - 1)
                    wait_past(act, up_ready, t - 2)
                    nc.scalar.activation(wh_t[:], wht_ps, ACT.Copy).then_inc(wht_read, 1)
                if has1:
                    act.wait_ge(tr_ready, t)
                    wait_past(act, down_ready, t - 1)
                    for kt in range(KT):
                        last = nc.scalar.activation(h_t[:, kt], tr_ps[:, kt], ACT.Identity, bias=mod[:, 2, kt:kt + 1],
                                                    scale=mod[:, 3, kt:kt + 1])
                    last.then_inc(h_ready, 1)
                if has0:
                    act.wait_ge(var_ready, t + 1)
                    nc.scalar.activation(std[:], var[:], ACT.Sqrt).then_inc(std_ready, 1)

            steps(act, step)

        @block.vector
        def _(dve):
            for kt in range(KT):
                dve.wait_ge(wo_hi_ready, kt + 1)
                nc.vector.tensor_tensor(wo_lo[:, kt], wo_raw[:, kt % 2], wo_hi[:, kt].bitcast(F32),
                                        ALU.subtract).then_inc(wo_split, 1)
            dve.wait_ge(small_in, 48)
            NORM_LINKS, ROUTE_LINKS = 9, 4

            class Chain:

                def __init__(self, which, base):
                    self.which, self.base, self.k = which, base, 0

                def link(self, ins):
                    self.k += 1
                    ins.then_inc(self.which, 1)

                def wait(self):
                    dve.wait_ge(self.which, self.base + self.k)

            def residual(t, r, pairs, half, norm):
                cols = slice(half * CH, (half + 1) * CH)
                dve.wait_ge(proj_ready, t * 2 + half + 1)
                if half == 0:
                    dve.wait_ge(x_in[r % 2], (pairs + 1) * 16)
                nc.vector.tensor_tensor(gated[:, cols], proj_ps[:, half], gates[:, 0, cols], ALU.mult).then_inc(proj_read, 1)
                dve.wait_ge(proj_read, t * 2 + half + 1)
                nc.vector.tensor_tensor(x1[:, r, cols], gated[:, cols], x_t[:, r % 2, cols], ALU.add).then_inc(x1_ready, 1)
                dve.wait_ge(x1_ready, t * 2 + half + 1)
                norm.link(nc.vector.bn_stats(stats[:, half], x1[:, r, cols]))

            def finish_norm(t, r, norm):
                norm.wait()
                norm.link(nc.vector.tensor_copy(cell[:], ident[:, 0:1]))
                norm.link(nc.vector.bn_aggr(meanvar[:], stats[:]))
                norm.wait()
                nc.vector.tensor_scalar_add(var[:], meanvar[:, 1:2], LN_EPS).then_inc(var_ready, 1)
                dve.wait_ge(std_ready, t + 1)
                norm.link(nc.vector.reciprocal(r0[:], std[:]))
                norm.wait()
                norm.link(nc.vector.tensor_tensor(r1[:], r0[:], r0[:], ALU.mult))
                norm.wait()
                norm.link(nc.vector.tensor_tensor(r2[:], r1[:], var[:], ALU.mult))
                norm.wait()
                norm.link(nc.vector.tensor_scalar(r1[:], r2[:], -0.5, 1.5, ALU.mult, ALU.add))
                norm.wait()
                norm.link(nc.vector.tensor_tensor(rstd[:], r0[:], r1[:], ALU.mult))
                norm.wait()
                assert norm.k == NORM_LINKS
                wait_past(dve, tr_ready, t)
                nc.vector.tensor_scalar(xn[:], x1[:, r], meanvar[:, 0:1], rstd[:], ALU.subtract, ALU.mult).then_inc(xn_ready, 1)

            def route_tile(t):
                c = Chain(chain1, t * ROUTE_LINKS)
                dve.wait_ge(down_ready, t + 1)
                logits = down_ps[:, 0:EXPERTS]
                c.link(nc.vector.tensor_reduce(top[:], logits, op=ALU.max, axis=AX.X))
                c.wait()
                c.link(nc.vector.scalar_tensor_tensor(out=rank[:], in0=logits, scalar=top[:], in1=ranks[:],
                                                      op0=ALU.is_equal, op1=ALU.mult))
                c.wait()
                c.link(nc.vector.tensor_reduce(top_rank[:], rank[:], op=ALU.max, axis=AX.X))
                c.wait()
                c.link(nc.vector.tensor_scalar(route[:], rank[:], top_rank[:], top[:], ALU.is_equal, ALU.mult))
                c.wait()
                assert c.k == ROUTE_LINKS
                wait_past(dve, wht_ready, t)
                nc.vector.tensor_tensor(wh[:].rearrange("p (e r) -> p e r", r=RANK),
                                        down_ps[:, EXPERTS:EXPERTS + ER].rearrange("p (e r) -> p e r", r=RANK),
                                        route[:].rearrange("p (e a) -> p e a", a=1).broadcast_to((P, EXPERTS, RANK)),
                                        ALU.mult).then_inc(wh_ready, 1)

            def output(t, r, pairs):
                dve.wait_ge(up_ready, t + 1)
                nc.vector.tensor_tensor(lora[:].rearrange("p (b n) -> p b n", b=2), up_ps,
                                        gates[:, 1].rearrange("p (b n) -> p b n", b=2), ALU.mult).then_inc(up_read, 1)
                dve.wait_ge(up_read, t + 1)
                wait_past(dve, y_out[r % 2], pairs * 16)
                nc.vector.tensor_tensor(y[:, r % 2], lora[:], x1[:, r], ALU.add).then_inc(y_ready, 1)

            def step(t, r, pairs, has0, has1, has2):
                norm = Chain(chain0, t * NORM_LINKS)
                if has0:
                    residual(t, r, pairs, 0, norm)
                if has2:
                    output(t - 2, (r - 2) % RING, pairs - 1)
                if has0:
                    residual(t, r, pairs, 1, norm)
                if has1:
                    route_tile(t - 1)
                if has0:
                    finish_norm(t, r, norm)

            steps(dve, step)

        @block.tensor
        def _(pe):
            def project(t, r, pairs, half):
                cols = slice(half * CH, (half + 1) * CH)
                if half == 0:
                    pe.wait_ge(o_in[r % 2], (pairs + 1) * 32)
                wait_past(pe, proj_read, (t - 1) * 2 + half + 1)
                for g in range(KVH):
                    if isinstance(t, int) and t == 0 and half == 0:
                        pe.wait_ge(wo_split, g + 1)
                    terms = ((o_hi[:, r % 2, g], wo_hi[:, g, cols]), (o_hi[:, r % 2, g], wo_lo[:, g, cols]),
                             (o_lo[:, r % 2, g], wo_hi[:, g, cols]))
                    for i, (lhs, rhs) in enumerate(terms):
                        last = nc.tensor.matmul(proj_ps[:, half], lhs, rhs, start=g == 0 and i == 0, stop=g == KVH - 1 and i == 2)
                last.then_inc(proj_ready, 1)

            def step(t, r, pairs, has0, has1, has2):
                if has0:
                    project(t, r, pairs, 0)
                if has2:
                    pe.wait_ge(wh_ready, t - 1)
                    wait_past(pe, wht_read, t - 2)
                    nc.tensor.transpose(wht_ps, wh[:], ident[:]).then_inc(wht_ready, 1)
                if has1:
                    pe.wait_ge(xn_ready, t)
                    wait_past(pe, h_ready, t - 1)
                    for kt in range(KT):
                        last = nc.tensor.transpose(tr_ps[:, kt], xn[:, kt * P:(kt + 1) * P], ident[:])
                    last.then_inc(tr_ready, 1)
                if has2:
                    if isinstance(t, int) and t == 2:
                        pe.wait_ge(small_in, 48)
                    pe.wait_ge(wht_read, t - 1)
                    wait_past(pe, up_read, t - 2)
                    for b in range(2):
                        last = nc.tensor.matmul(up_ps[:, b], wh_t[:], up[:, b * CH:(b + 1) * CH], start=True, stop=True)
                    last.then_inc(up_ready, 1)
                if has0:
                    project(t, r, pairs, 1)
                if has1:
                    if isinstance(t, int) and t == 1:
                        pe.wait_ge(small_in, 48)
                    pe.wait_ge(h_ready, t)
                    wait_past(pe, wh_ready, t - 1)
                    for kt in range(KT):
                        last = nc.tensor.matmul(down_ps[:, 0:EXPERTS + ER], h_t[:, kt], down[:, kt], start=kt == 0, stop=kt == KT - 1)
                    last.then_inc(down_ready, 1)

            steps(pe, step)


def build_program(nc, io, out):
    io = dict(io, out=out)
    S = {
        "gates": nc.dram_tensor("gate_rows", [2, D], F32, kind="Internal").ap(),
        "q": nc.dram_tensor("q_split", [2, 2, HEADS, HALF, T], F32, kind="Internal").ap(),
        "k": nc.dram_tensor("k_split", [2, 2, KVH, HALF, T], F32, kind="Internal").ap(),
        "o": nc.dram_tensor("attention_split", [2, KVH, P, T], F32, kind="Internal").ap(),
    }
    ctx = ExitStack()
    with ctx:
        def sb(name, shape, dt=F32):
            return ctx.enter_context(nc.sbuf_tensor(name, shape, dt))

        M = {
            "ident": sb("identity", [P, P]),
            "ranks": sb("expert_ranks", [P, EXPERTS]),
            "masks": sb("masks_bf16", [P, 3, P], BF16),
            "mod": sb("modulation", [P, 4, KT]),
            "c_act": sb("silu_c", [P, KT, HD]),
            "pick": sb("pick_row", [P, 1]),
            "psum": ctx.enter_context(nc.psum_tensor("psum_banks", [P, 8, CH], F32)),
        }
        with ExitStack() as upto_attend:
            M["v_all"] = upto_attend.enter_context(nc.sbuf_tensor("v_all", [P, NTT, KV_W], F32))
            with ExitStack() as upto_project:
                M["w_hi"] = upto_project.enter_context(nc.sbuf_tensor("w_hi", [P, KT, WCOLS], F32R))
                M["w_lo"] = upto_project.enter_context(nc.sbuf_tensor("w_lo", [P, KT, WCOLS], F32R))
                M["x"] = upto_project.enter_context(nc.sbuf_tensor("x_chunk", [P, TPC, D], F32))
                M["x_in"] = [upto_project.enter_context(nc.semaphore(f"x_in{j}")) for j in range(TPC)]
                modulate_block(nc, io, S, M)
                project_block(nc, io, S, M)
            attend_block(nc, io, S, M)
        feed_block(nc, io, S, M)


def shape_constants():
    base = np.float32(500000.0)
    exponent = np.arange(0, HD, 2, dtype=np.float32) / np.float32(HD)
    inv_freq = np.float32(1.0) / np.power(np.float64(base), exponent.astype(np.float64)).astype(np.float32)
    angle = np.arange(T, dtype=np.float32)[None, :] * inv_freq[:, None]
    trig = np.stack([np.cos(angle), np.sin(angle)], axis=1).astype(np.float32)
    trig = np.ascontiguousarray(np.tile(trig, (P // HALF, 1, 1)))
    consts = np.zeros((P, P + EXPERTS), np.float32)
    consts[:, :P] = np.eye(P)
    consts[:, P:] = EXPERTS - np.arange(EXPERTS)
    row, col = np.arange(P)[:, None], np.arange(P)[None, :]
    masks = np.stack([np.eye(P), np.where(col > row, MASKED, 0.0), np.where(row > col, MASKED, 0.0)], axis=1)
    return trig, consts, masks.astype(mybir.dt.np(BF16))


def kernel(**inputs):
    import concourse.bacc as bacc
    from concourse.bass_utils import run_bass_kernel_spmd

    a = {k: np.asarray(v) for k, v in inputs.items()}
    trig, consts, masks = shape_constants()
    wq = a["L0_attn_Wq"].reshape(D, QUNITS, HPU, 2, HALF).transpose(0, 1, 3, 2, 4).reshape(D, HEADS * HD)
    wk = a["L0_attn_Wk"].reshape(D, KVH, 2, HALF).transpose(0, 2, 1, 3).reshape(D, KV_W)
    arrays = {
        "x": a["L0_attn_x"].reshape(T, D),
        "wqkv": np.concatenate([wk, a["L0_attn_Wv"], wq], axis=1),
        "wo": a["L0_attn_Wo"],
        "down": np.concatenate([a["L0_ffn_route_w"], a["L0_ffn_A"].reshape(ER, D)], axis=0).T,
        "up": a["L0_ffn_Bw"].transpose(0, 2, 1).reshape(ER, D),
        "c": a["L0_c"],
        "wmod": a["L0_wmod"],
        "trig": trig,
        "consts": consts,
        "masks": masks,
    }
    nc = bacc.Bacc("TRN2", target_bir_lowering=False, num_devices=1)
    feeds, io = {}, {}
    for name, array in arrays.items():
        array = np.ascontiguousarray(array)
        feeds[f"in_{name}"] = array
        io[name] = nc.dram_tensor(f"in_{name}", array.shape, mybir.dt.from_np(array.dtype), kind="ExternalInput").ap()
    out = nc.dram_tensor("out_x", (T, D), F32, kind="ExternalOutput").ap()
    build_program(nc, io, out)
    result = run_bass_kernel_spmd(nc, [feeds], core_ids=[0])
    return result.results[0]["out_x"].reshape(1, T, D)
```

```python
from contextlib import ExitStack

import numpy as np

import concourse.bass as bass
from concourse import mybir

F32 = mybir.dt.float32
F32R = mybir.dt.float32r
BF16 = mybir.dt.bfloat16
ALU = mybir.AluOpType
ACT = mybir.ActivationFunctionType
AX = mybir.AxisListType

P = 128
T, D = 2048, 1024
HEADS, KVH, HD = 32, 8, 32
GRP = HEADS // KVH
HALF = HD // 2
KT = D // P
CH = 512
NCH = T // CH
TPC = CH // P
NTT = T // P
EXPERTS, RANK = 8, 16
ER = EXPERTS * RANK
LN_EPS = 1e-5
SCORE_SCALE = float(HD) ** -0.5
MASKED = -1e30

KV_W = KVH * HD
COL_K, COL_V, COL_Q = 0, KV_W, 2 * KV_W
WCOLS = COL_Q + HEADS * HD
HPU = P // HALF
QUNITS = HEADS // HPU
UNITS = 2 + QUNITS
ROPES = 1 + QUNITS

MODC = 256
MPP = D // MODC
MOD_RING = 4
NP = 8
SIDE = 4


def wait_past(eng, sem, value):
    if not isinstance(value, int) or value > 0:
        eng.wait_ge(sem, value)


def multiply_piece(nc, rows_ps, piece, c_act):
    for kk in range(KT):
        at = kk % SIDE * HD
        last = nc.tensor.matmul(rows_ps[at:at + HD], c_act[:, kk], piece[:, kk], start=kk < SIDE, stop=kk >= KT - SIDE)
    return last


def turn_piece(nc, cols_ps, rows, pick, at):
    for half in range(MODC // P):
        last = nc.tensor.matmul(cols_ps[:, at + half:at + half + 1], rows[:, half * P:(half + 1) * P], pick[:], start=True, stop=True)
    return last


def modulate_block(nc, io, S, M):
    ctx = ExitStack()
    with ctx:
        def sb(name, shape, dt=F32):
            return ctx.enter_context(nc.sbuf_tensor(name, shape, dt))

        def sem(name):
            return ctx.enter_context(nc.semaphore(name))

        c_col = sb("c_col", [P, KT])
        c_exp = sb("c_exp", [P, KT])
        c_den = sb("c_den", [P, KT])
        c_rec = sb("c_rec", [P, KT])
        piece = sb("wmod_piece", [P, MOD_RING, KT, MODC])
        wraw = sb("w_raw", [P, 2, WCOLS])
        rows = sb("mod_rows", [P, 2, MODC])
        cols_ps = M["psum"][:, 0, :]
        rows_ps = M["psum"][:, 1:3, 0:MODC]
        PIECES = 2 * MPP
        assert PIECES == KT

        c_in = sem("c_in")
        const_in = sem("const_in")
        piece_in = [sem(f"piece_in{i}") for i in range(MOD_RING)]
        piece_used = sem("piece_used")
        w_in = [sem(f"w_in{i}") for i in range(2)]
        w_hi_done = sem("w_hi_done")
        w_split = sem("w_split")
        exp_ready = sem("exp_ready")
        act_ready = sem("c_act_ready")
        chain = sem("mod_chain")
        pick_ready = sem("pick_ready")
        rows_copied = sem("rows_copied")
        turned = sem("rows_turned")
        block = ctx.enter_context(nc.Block())

        @block.sync
        def _(sp):
            sp.dma_start(c_col[:], io["c"].rearrange("a (p kk) -> (a p) kk", kk=KT)).then_inc(c_in, 16)
            sp.dma_start(M["ident"][:], io["consts"][:, 0:P]).then_inc(const_in, 16)
            sp.dma_start(M["ranks"][:], io["consts"][:, P:P + EXPERTS]).then_inc(const_in, 16)
            sp.dma_start(M["masks"][:], io["masks"]).then_inc(const_in, 16)
            wmod_v = io["wmod"].rearrange("(p kk) n -> p kk n", kk=KT)
            for n in range(PIECES):
                wait_past(sp, piece_used, n - MOD_RING + 1)
                sp.dma_start(piece[:, n % MOD_RING], wmod_v[:, :, n * MODC:(n + 1) * MODC]).then_inc(piece_in[n % MOD_RING], 16)
            for j in range(TPC):
                sp.dma_start(M["x"][:, j], io["x"][j * P:(j + 1) * P, :]).then_inc(M["x_in"][j], 16)

        @block.scalar
        def _(act):
            def load(kt):
                wait_past(act, w_split, kt - 1)
                act.dma_start(wraw[:, kt % 2], io["wqkv"][kt * P:(kt + 1) * P, :]).then_inc(w_in[kt % 2], 16)

            load(0)
            load(1)
            act.wait_ge(c_in, 16)
            nc.scalar.activation(c_exp[:], c_col[:], ACT.Exp, scale=-1.0).then_inc(exp_ready, 1)
            for kt in range(KT):
                act.wait_ge(w_in[kt % 2], 16 * (kt // 2 + 1))
                nc.scalar.activation(M["w_hi"][:, kt], wraw[:, kt % 2], ACT.Copy).then_inc(w_hi_done, 1)
                if kt + 2 < KT:
                    load(kt + 2)

        @block.vector
        def _(dve):
            done = 0

            def link(ins):
                nonlocal done
                done += 1
                ins.then_inc(chain, 1)
                dve.wait_ge(chain, done)

            dve.wait_ge(exp_ready, 1)
            link(nc.vector.tensor_scalar_add(c_den[:], c_exp[:], 1.0))
            link(nc.vector.reciprocal(c_rec[:], c_den[:]))
            def wide(col):
                return col[:].rearrange("p (k a) -> p k a", a=1).broadcast_to((P, KT, HD))

            nc.vector.tensor_tensor(M["c_act"][:], wide(c_col), wide(c_rec), ALU.mult).then_inc(act_ready, 1)
            dve.wait_ge(const_in, 48)
            nc.vector.tensor_reduce(M["pick"][:], M["ident"][:, 0:P:HD], op=ALU.add, axis=AX.X).then_inc(pick_ready, 1)
            for kt in range(KT):
                dve.wait_ge(w_hi_done, kt + 1)
                nc.vector.tensor_tensor(M["w_lo"][:, kt], wraw[:, kt % 2], M["w_hi"][:, kt].bitcast(F32),
                                        ALU.subtract).then_inc(w_split, 1)
                dve.wait_ge(piece_used, kt + 1)
                wait_past(dve, turned, kt - 1)
                nc.vector.tensor_copy(rows[:, kt % 2], rows_ps[:, kt % 2]).then_inc(rows_copied, 1)
            dve.wait_ge(turned, PIECES)
            nc.vector.tensor_copy(M["mod"][:, 0, :], cols_ps[:, 0:KT])
            nc.vector.tensor_scalar_add(M["mod"][:, 1, :], cols_ps[:, KT:2 * KT], 1.0)

        @block.tensor
        def _(pe):
            pe.wait_ge(act_ready, 1)
            for n in range(PIECES):
                pe.wait_ge(piece_in[n % MOD_RING], 16 * (n // MOD_RING + 1))
                wait_past(pe, rows_copied, n - 1)
                multiply_piece(nc, rows_ps[:, n % 2], piece[:, n % MOD_RING], M["c_act"]).then_inc(piece_used, 1)
                if n == 0:
                    pe.wait_ge(pick_ready, 1)
                else:
                    pe.wait_ge(rows_copied, n)
                    turn_piece(nc, cols_ps, rows[:, (n - 1) % 2], M["pick"], (n - 1) * (MODC // P)).then_inc(turned, 1)
            pe.wait_ge(rows_copied, PIECES)
            turn_piece(nc, cols_ps, rows[:, (PIECES - 1) % 2], M["pick"], (PIECES - 1) * (MODC // P)).then_inc(turned, 1)


def project_block(nc, io, S, M):
    ctx = ExitStack()
    with ctx:
        def sb(name, shape, dt=F32):
            return ctx.enter_context(nc.sbuf_tensor(name, shape, dt))

        def sem(name):
            return ctx.enter_context(nc.semaphore(name))

        x = M["x"]
        xn = sb("x_normed", [P, TPC, D])
        hf = sb("h_full", [P, 2, CH])
        h_hi = sb("h_hi", [P, KT, CH], F32R)
        h_lo = sb("h_lo", [P, KT, CH], F32R)
        trig = sb("trig", [P, 2, CH])
        by_cos = sb("by_cos", [P, 2, CH])
        by_sin = sb("by_sin", [P, 2, CH])
        rot = sb("rotated", [P, 2, CH])
        rot_hi = sb("rotated_hi", [P, 2, CH], F32R)
        rot_lo = sb("rotated_lo", [P, 2, CH], F32R)
        stats = sb("ln_stats", [P, TPC, 2, 6])
        meanvar = sb("ln_meanvar", [P, TPC, 2])
        var = sb("ln_var", [P, TPC])
        std = sb("ln_std", [P, TPC])
        cell = sb("hold_cell", [P, 1])
        r0 = sb("ln_r0", [P, TPC])
        r1 = sb("ln_r1", [P, TPC])
        r2 = sb("ln_r2", [P, TPC])
        rstd = sb("ln_rstd", [P, TPC])
        w_hi, w_lo, ident, mod, v_all = M["w_hi"], M["w_lo"], M["ident"], M["mod"], M["v_all"]
        unit_ps = M["psum"][:, 0:4].rearrange("p (s b) n -> p s b n", s=2)
        tr_ps = M["psum"][:, 4:8]

        x_in = M["x_in"]
        trig_in = sem("trig_in")
        var_ready = sem("var_ready")
        std_ready = sem("std_ready")
        xn_ready = sem("xn_ready")
        tr_ready = sem("tr_ready")
        hf_ready = sem("hf_ready")
        hh_ready = sem("hh_ready")
        h_ready = sem("h_ready")
        unit_ready = sem("unit_ready")
        v_read = sem("v_read")
        rope_read = sem("rope_read")
        rot_ready = sem("rot_ready")
        hi_ready = sem("hi_ready")
        lo_ready = sem("lo_ready")
        hi_out = sem("hi_out")
        lo_out = sem("lo_out")
        chain = sem("proj_chain")
        block = ctx.enter_context(nc.Block())

        q_dram, k_dram = S["q"], S["k"]

        @block.sync
        def _(sp):
            def load_x(n, j):
                sp.dma_start(x[:, j], io["x"][bass.ds(n * CH + j * P, P), :]).then_inc(x_in[j], 16)

            def chunk(n, first, last):
                if not first:
                    sp.wait_ge(rope_read, n * ROPES)
                sp.dma_start(trig[:], io["trig"][:, :, bass.ds(n * CH, CH)]).then_inc(trig_in, 16)
                if not last:
                    for j in range(TPC):
                        sp.wait_ge(xn_ready, n * TPC + j + 1)
                        load_x(n + 1, j)
                for r in range(ROPES):
                    for part, tile, ready, out in ((0, rot_hi, hi_ready, hi_out), (1, rot_lo, lo_ready, lo_out)):
                        sp.wait_ge(ready, n * ROPES + r + 1)
                        for b in range(2):
                            heads = slice(0, KVH) if r == 0 else slice((r - 1) * HPU, r * HPU)
                            dst = (k_dram if r == 0 else q_dram)[part, b, heads, :, bass.ds(n * CH, CH)]
                            sp.dma_start(dst.rearrange("h i t -> (h i) t"), tile[:, b].bitcast(F32)).then_inc(out, 16)

            chunk(0, True, False)
            with sp.Fori(1, NCH - 1) as n:
                chunk(n, False, False)
            chunk(NCH - 1, False, True)
            sp.wait_ge(hi_out, NCH * ROPES * 32)
            sp.wait_ge(lo_out, NCH * ROPES * 32)

        @block.scalar
        def _(act):
            def sqrt_of_var(n):
                act.wait_ge(var_ready, n + 1)
                nc.scalar.activation(std[:], var[:], ACT.Sqrt).then_inc(std_ready, 1)

            def rope_hi(n, r, first):
                act.wait_ge(rot_ready, n * ROPES + r + 1)
                if not (first and r == 0):
                    act.wait_ge(hi_out, (n * ROPES + r) * 32)
                nc.scalar.activation(rot_hi[:], rot[:], ACT.Copy).then_inc(hi_ready, 1)

            def chunk(n, first, last):
                for kt in range(KT):
                    act.wait_ge(tr_ready, n * KT + kt + 1)
                    if not (first and kt < 2):
                        act.wait_ge(h_ready, n * KT + kt - 1)
                    nc.scalar.activation(hf[:, kt % 2], tr_ps[:, kt % 4], ACT.Identity, bias=mod[:, 0, kt:kt + 1],
                                         scale=mod[:, 1, kt:kt + 1]).then_inc(hf_ready, 1)
                if not last:
                    sqrt_of_var(n + 1)
                rope_hi(n, 0, first)
                act.wait_ge(unit_ready, n * UNITS + 2)
                nc.scalar.activation(v_all[:, bass.ds(n * TPC, TPC), :], unit_ps[:, 1].rearrange("p b (j c) -> p (b j) c", j=2),
                                     ACT.Copy).then_inc(v_read, 1)
                for r in range(1, ROPES):
                    rope_hi(n, r, first)

            sqrt_of_var(0)
            chunk(0, True, False)
            with act.Fori(1, NCH - 1) as n:
                chunk(n, False, False)
            chunk(NCH - 1, False, True)

        @block.vector
        def _(dve):
            LINKS = TPC * 3 + 6

            def norm(n, first):
                base = n * LINKS
                k = 0

                def link(ins):
                    nonlocal k
                    k += 1
                    ins.then_inc(chain, 1)

                for j in range(TPC):
                    dve.wait_ge(x_in[j], (n + 1) * 16)
                    for half in range(2):
                        link(nc.vector.bn_stats(stats[:, j, half], x[:, j, half * CH:(half + 1) * CH]))
                dve.wait_ge(chain, base + k)
                link(nc.vector.tensor_copy(cell[:], ident[:, 0:1]))
                for j in range(TPC):
                    link(nc.vector.bn_aggr(meanvar[:, j], stats[:, j]))
                dve.wait_ge(chain, base + k)
                nc.vector.tensor_scalar_add(var[:], meanvar[:, :, 1], LN_EPS).then_inc(var_ready, 1)
                dve.wait_ge(std_ready, n + 1)
                link(nc.vector.reciprocal(r0[:], std[:]))
                dve.wait_ge(chain, base + k)
                link(nc.vector.tensor_tensor(r1[:], r0[:], r0[:], ALU.mult))
                dve.wait_ge(chain, base + k)
                link(nc.vector.tensor_tensor(r2[:], r1[:], var[:], ALU.mult))
                dve.wait_ge(chain, base + k)
                link(nc.vector.tensor_scalar(r1[:], r2[:], -0.5, 1.5, ALU.mult, ALU.add))
                dve.wait_ge(chain, base + k)
                link(nc.vector.tensor_tensor(rstd[:], r0[:], r1[:], ALU.mult))
                dve.wait_ge(chain, base + k)
                assert k == LINKS
                if not first:
                    dve.wait_ge(tr_ready, n * KT)
                for j in range(TPC):
                    nc.vector.tensor_scalar(xn[:, j], x[:, j], meanvar[:, j, 0:1], rstd[:, j:j + 1],
                                            ALU.subtract, ALU.mult).then_inc(xn_ready, 1)

            def split_lo(n, r, first):
                dve.wait_ge(hi_ready, n * ROPES + r + 1)
                if not (first and r == 0):
                    dve.wait_ge(lo_out, (n * ROPES + r) * 32)
                nc.vector.tensor_tensor(rot_lo[:], rot[:], rot_hi[:].bitcast(F32), ALU.subtract).then_inc(lo_ready, 1)

            def chunk(n, first, last):
                for kt in range(KT):
                    dve.wait_ge(hf_ready, n * KT + kt + 1)
                    if not first and kt == 0:
                        dve.wait_ge(unit_ready, n * UNITS)
                    nc.vector.tensor_copy(h_hi[:, kt], hf[:, kt % 2]).then_inc(hh_ready, 1)
                    dve.wait_ge(hh_ready, n * KT + kt + 1)
                    nc.vector.tensor_tensor(h_lo[:, kt], hf[:, kt % 2], h_hi[:, kt].bitcast(F32),
                                            ALU.subtract).then_inc(h_ready, 1)
                if not last:
                    norm(n + 1, False)
                dve.wait_ge(trig_in, (n + 1) * 16)
                for r in range(ROPES):
                    unit = 0 if r == 0 else r + 1
                    dve.wait_ge(unit_ready, n * UNITS + unit + 1)
                    if not (first and r == 0):
                        dve.wait_ge(rot_ready, n * ROPES + r)
                    for tile, f in ((by_cos, 0), (by_sin, 1)):
                        table = trig[:, f:f + 1, :].broadcast_to((P, 2, CH))
                        last_ins = nc.vector.tensor_tensor(tile[:], unit_ps[:, unit % 2], table, ALU.mult)
                    last_ins.then_inc(rope_read, 1)
                    if r:
                        split_lo(n, r - 1, first)
                split_lo(n, ROPES - 1, False)

            norm(0, True)
            chunk(0, True, False)
            with dve.Fori(1, NCH - 1) as n:
                chunk(n, False, False)
            chunk(NCH - 1, False, True)

        @block.gpsimd
        def _(pool):
            def chunk(n, first):
                for r in range(ROPES):
                    pool.wait_ge(rope_read, n * ROPES + r + 1)
                    if not (first and r == 0):
                        pool.wait_ge(lo_ready, n * ROPES + r)
                    nc.gpsimd.tensor_tensor(rot[:, 0], by_cos[:, 0], by_sin[:, 1], ALU.subtract)
                    nc.gpsimd.tensor_tensor(rot[:, 1], by_sin[:, 0], by_cos[:, 1], ALU.add).then_inc(rot_ready, 1)

            chunk(0, True)
            with pool.Fori(1, NCH) as n:
                chunk(n, False)

        @block.tensor
        def _(pe):
            def products(out, terms, start, stop):
                for i, (lhs, rhs) in enumerate(terms):
                    last = nc.tensor.matmul(out, lhs, rhs, start=start and i == 0, stop=stop and i == len(terms) - 1)
                return last

            def chunk(n, first):
                pe.wait_ge(xn_ready, (n + 1) * TPC)
                for kt in range(KT):
                    if not (first and kt < 4):
                        pe.wait_ge(hf_ready, n * KT + kt - 3)
                    for j in range(TPC):
                        last = nc.tensor.transpose(tr_ps[:, kt % 4, j * P:(j + 1) * P], xn[:, j, kt * P:(kt + 1) * P], ident[:])
                    last.then_inc(tr_ready, 1)
                for unit in range(UNITS):
                    if unit == 3:
                        pe.wait_ge(v_read, n + 1)
                    elif not (first and unit < 2):
                        pe.wait_ge(rope_read, n * ROPES + {0: -1, 1: 0, 2: 1, 4: 2, 5: 3}[unit])
                    if unit == 1:
                        for j in range(TPC):
                            out = unit_ps[:, 1, j // 2, (j % 2) * KV_W:(j % 2 + 1) * KV_W]
                            rows, cols = slice(j * P, (j + 1) * P), slice(COL_V, COL_V + KV_W)
                            for kt in range(KT):
                                last = products(out, ((h_hi[:, kt, rows], w_hi[:, kt, cols]), (h_hi[:, kt, rows], w_lo[:, kt, cols]),
                                                      (h_lo[:, kt, rows], w_hi[:, kt, cols])), kt == 0, kt == KT - 1)
                    else:
                        at = COL_K if unit == 0 else COL_Q + (unit - 2) * 2 * P
                        for kt in range(KT):
                            if unit == 0:
                                pe.wait_ge(h_ready, n * KT + kt + 1)
                            for b in range(2):
                                cols = slice(at + b * P, at + (b + 1) * P)
                                last = products(unit_ps[:, unit % 2, b], ((w_hi[:, kt, cols], h_hi[:, kt]), (w_hi[:, kt, cols], h_lo[:, kt]),
                                                                          (w_lo[:, kt, cols], h_hi[:, kt])), kt == 0, kt == KT - 1)
                    last.then_inc(unit_ready, 1)

            chunk(0, True)
            with pe.Fori(1, NCH) as n:
                chunk(n, False)


def attend_block(nc, io, S, M):
    ctx = ExitStack()
    with ctx:
        def sb(name, shape, dt=F32):
            return ctx.enter_context(nc.sbuf_tensor(name, shape, dt))

        def sem(name):
            return ctx.enter_context(nc.semaphore(name))

        piece = M["wmod_piece2"]
        probs = M["probs"]
        gate_col = sb("gate_col", [P, 2, KT])
        gate_neg = sb("gate_neg", [P, 2, KT])
        gate_abs = sb("gate_abs", [P, 2, KT])
        gate_sgn = sb("gate_sgn", [P, 2, KT])
        gate_fin = sb("gate_fin", [P, 2, KT])
        gate_row = sb("gate_row", [2 * KT, P])
        mod_rows = sb("mod_rows2", [P, 2, MODC])
        PIECES = range(2 * MPP, 6 * MPP)
        GA_AT, SB_AT, CB_AT, GB_AT = 0, KT, 2 * KT, 3 * KT
        ONES_ROW = 3 * HD
        qs = [M["q_stack0"], sb("q_stack1", [ONES_ROW + 1, NCH, GRP, CH], F32R)]
        ks = [sb(f"k_stack{u}", [ONES_ROW + 1, T], F32R) for u in range(2)]
        v_g = [sb(f"v_group{u}", [P, NTT, HD]) for u in range(2)]
        sums = sb("prob_sums", [P, 2, GRP, CH])
        part_max = sb("part_max", [P, NTT, NCH + 1, GRP])
        CHUNKS_OF = [range(0, NCH - 2), range(NCH - 2, NCH - 1), range(NCH - 1, NCH)]
        PARTS = len(CHUNKS_OF)
        q_max = sb("q_max", [P, PARTS, P])
        neg_max = [sb(f"neg_max{part}", [len(CHUNKS_OF[part]) * GRP * TPC, P], F32R) for part in range(PARTS)]
        ones = sb("ones_sum", [P, HD])
        o_raw = sb("o_raw", [P, 2, CH])
        o_sum = sb("o_sum", [P, 2, CH])
        SPREAD = GRP * CH // P
        few_sum = sb("few_sum", [P, SPREAD])
        few_rec = sb("few_rec", [P, SPREAD])
        o_rec = sb("o_rec", [P, CH])
        o_full = sb("o_full", [P, CH])
        o_hi = sb("o_hi", [P, CH], F32R)
        o_lo = sb("o_lo", [P, CH], F32R)
        ident, masks, v_all = M["ident"], M["masks"], M["v_all"]
        ident_b, mask_qk, mask_kq = masks[:, 0], masks[:, 1], masks[:, 2]

        def four(mask):
            return mask.rearrange("p (a t) -> p a t", a=1).broadcast_to((P, GRP, P))

        max_ps = M["psum"][:, 0:4].rearrange("p (s b) n -> p s b n", s=2)
        score_ps = M["psum"][:, 4:6]
        out_ps = M["psum"][:, 6]
        sum_ps = M["psum"][:, 7]
        rows_ps = M["psum"][:, 6:8, 0:MODC]

        STEPS = [(c, kb) for c in range(NCH) for kb in range((c + 1) * TPC)]
        LAST = [max(n for n, st in enumerate(STEPS) if st[0] == c) for c in range(NCH)]
        NS = len(STEPS)

        def score_units(n):
            c, kb = STEPS[n]
            if kb < c * TPC:
                return [((j, j + 1), (0, CH), False) for j in range(GRP)]
            off = kb * P - c * CH
            out, rest = [((0, GRP), (off, off + P), True)], CH - off - P
            if rest:
                k = min(GRP, CH // rest)
                k = {1: 1, 2: 2, 4: 4}[k]
                out += [((j, j + k), (off + P, CH), False) for j in range(0, GRP, k)]
            return out

        UNITS_OF = [score_units(n) for n in range(NS)]
        BEFORE = [sum(len(u) for u in UNITS_OF[:n]) for n in range(NS + 1)]
        NU = BEFORE[NS]
        assert NU % 2 == 0 and NS % NP == 0

        ADDED_IN_PASS = [[], [0, 1, 2, 3], [0, 1, 2, 4, 5, 6, 7, 8], [0, 1, 2, 4, 5, 6, 8, 9, 10, 12]]
        ADDED_IN_LAST = [[], [0, 1, 2, 3], [0, 1, 2, 4, 6, 7], [0, 2, 4, 6, 8, 10]]
        NADD = sum(max(0, len(a) - 1) for a in ADDED_IN_PASS)

        def added_up(last):
            tiles = ADDED_IN_LAST if last else ADDED_IN_PASS
            return tiles, [max(0, len(a) - 1) for a in tiles]

        def add_after(last, c, kb):
            tiles, adds = added_up(last)
            return sum(adds[:c]) + max(1, tiles[c].index(kb))

        def max_units():
            out = []
            for qb in range(NTT):
                c, r = divmod(qb, TPC)
                for kc in range(c):
                    for hp in range(2):
                        out.append((qb, kc, [(b, 0, 2 * hp + b, kc * CH, CH) for b in range(2)], None, ("pair", hp, CH)))
                diag = [(0, j * P, j, qb * P, P) for j in range(GRP)]
                if r == 1:
                    out.append((qb, c, diag + [(1, j * P, j, c * CH, P) for j in range(GRP)], 0, ("both", 0, P)))
                    continue
                out.append((qb, c, diag, 0, ("diag", 0, P)))
                if r == 2:
                    out.append((qb, c + 1, [(j // 2, j % 2 * 2 * P, j, c * CH, 2 * P) for j in range(GRP)], None, ("four", 0, 2 * P)))
                if r == 3:
                    for hp in range(2):
                        out.append((qb, c + 1, [(b, 0, 2 * hp + b, c * CH, 3 * P) for b in range(2)], None, ("pair", hp, 3 * P)))
            return out

        MAXES = max_units()
        NM = len(MAXES)
        assert NM % 2 == 0 and NM // 2 > TPC
        FIRST_OF_CHUNK = [min(m for m in range(NM) if MAXES[m][0] >= c * TPC) for c in range(NCH)]
        END_OF_PART = [max(m for m in range(NM) if MAXES[m][0] // TPC in CHUNKS_OF[part]) + 1 for part in range(PARTS)]
        TURN = [NM + part for part in range(PARTS)]
        EARLY = 37
        OWN_PLAN = [(EARLY, END_OF_PART[1], 0, 6), (END_OF_PART[1], NM, 7, 20)]
        NEXT_PLAN = [(0, END_OF_PART[0], 21, 30), (END_OF_PART[0], EARLY, 31, 37)]
        COPY_V = 5
        LOADS = 12
        REST_LOADS = LOADS // 2 * NCH
        FIRST_PIECE = 9
        LAG = 2
        REC_LAG, NORM_LAG = 4, 6

        piece_in = [sem(f"piece2_in{i}") for i in range(MOD_RING)]
        piece_used = sem("piece2_used")
        rows_copied = sem("rows2_copied")
        rows_turned = sem("rows2_turned")
        wo_hi_ready = sem("wo_hi_ready")
        mod_chain = sem("gate_chain")
        gate_ready = sem("gate_ready")
        gate_turned = sem("gate_turned")
        gate_out = sem("gate_out")
        first_in = [sem(f"first_load_in{c}") for c in range(2)]
        load_in = [sem(f"load_in{u}") for u in range(2)]
        negmax_in = [sem(f"negmax_in{u}") for u in range(2)]
        ones_ready = sem("ones_ready")
        v_ready = sem("v_ready")
        score_ready = sem("score_ready")
        prob_ready = sem("prob_ready")
        step_done = sem("step_done")
        max_ready = sem("max_ready")
        max_read = sem("max_read")
        qmax_ready = sem("qmax_ready")
        maxt_ready = sem("maxt_ready")
        negmax_ready = sem("negmax_ready")
        sum_added = sem("sum_added")
        raw_ready = sem("raw_ready")
        sum_in = sem("few_sum_in")
        rec_ready = sem("few_rec_ready")
        rec_out = sem("rec_out")
        rec_in = sem("rec_in")
        o_ready = sem("o_ready")
        hi_ready = sem("o_hi_ready")
        split_ready = sem("o_split_ready")
        o_out = sem("o_out")
        block = ctx.enter_context(nc.Block())

        PLACES = [[], [2], [0, 2], [0, 1, 2], [0, 1, 2, 2]]
        PLACES_SUMS = [[], [0], [0, 3], [0, 1, 3], [0, 1, 2, 3]]

        def passes(eng, one):
            one(0, 0, False, True)
            one(0, 0, True, True)
            with eng.Fori(0, (KVH - 2) // 2) as i:
                one(i, 1, True, True)
                one(i + 1, 0, True, True)
            one(KVH // 2 - 1, 1, True, False)

        def load_stacks(eng, which, g, v, c0, c1, loaded):
            cols = slice(c0 * CH, c1 * CH)
            for block_of_rows, q_part, k_part in ((0, 0, 0), (1, 0, 1), (2, 1, 0)):
                for b in range(2):
                    at = block_of_rows * HD + b * HALF
                    if "k" in which:
                        eng.dma_start(ks[v][at:at + HALF, cols].bitcast(F32),
                                      S["k"][k_part, b, bass.ds(g, 1), :, cols].rearrange("a i t -> (a i) t")).then_inc(loaded, 16)
                    if "q" in which:
                        eng.dma_start(qs[v][at:at + HALF, c0:c1].bitcast(F32),
                                      S["q"][q_part, b, bass.ds(g * GRP, GRP), :, cols].rearrange("j i (c t) -> i c j t", t=CH))\
                           .then_inc(loaded, 16)

        WIDE_FROM = BEFORE[LAST[NCH - 2] + 1]
        WIDE_BANKS = [4 + WIDE_FROM % 2, 5 - WIDE_FROM % 2, 0, 1, 2, 3]

        def unit_view(unit, heads, width, last):
            bank = WIDE_BANKS[(unit - WIDE_FROM) % len(WIDE_BANKS)] if last and unit >= WIDE_FROM else 4 + unit % 2
            return M["psum"][:, bank, 0:heads * width].rearrange("p (j t) -> p j t", j=heads)

        def after(h, u, weigh):
            if not weigh:
                return h, u
            return (h, 1) if u == 0 else (h + 1, 0)

        def spread(units, steps, out):
            lo, hi = steps
            work = [GRP * (CH - max(0, kb * P - c * CH)) for c, kb in STEPS]
            size = [sum(p[4] for p in MAXES[m][2]) for m in units]
            seen, done, n = 0, work[lo], lo
            for m, part in zip(units, size):
                while seen * sum(work[lo:hi]) >= done * sum(size):
                    n += 1
                    done += work[n]
                out[n].append(m)
                seen += part

        def schedule(weigh, maxima):
            own, following = [[] for _ in STEPS], [[] for _ in STEPS]
            if not weigh:
                return own[:1], [[*range(END_OF_PART[0]), TURN[0], *range(END_OF_PART[0], EARLY)]]
            for plan, out in ((OWN_PLAN, own), (NEXT_PLAN if maxima else [], following)):
                for first, end, lo, hi in plan:
                    spread(range(first, end), (lo, hi), out)
                    if end in END_OF_PART:
                        out[hi].append(TURN[END_OF_PART.index(end)])
            return own, following

        @block.sync
        def _(sp):
            def store(s, c):
                sp.wait_ge(split_ready, s * NCH + c + 1)
                for part, tile in ((0, o_hi), (1, o_lo)):
                    sp.dma_start(S["o"][part, bass.ds(s, 1), :, c * CH:(c + 1) * CH].rearrange("a p t -> (a p) t"),
                                 tile[:].bitcast(F32)).then_inc(o_out, 16)

            def reciprocals(s, c):
                n = s * NCH + c
                sp.wait_ge(raw_ready, n + 1)
                for j in range(GRP):
                    rows = slice(j * HD, (j + 1) * HD)
                    sp.dma_start(few_sum[rows], o_sum[j * HD:j * HD + 1, c % 2].rearrange("a (p t) -> a p t", t=SPREAD)).then_inc(sum_in, 16)
                sp.wait_ge(rec_ready, n + 1)
                sp.dma_start(S["rec"].rearrange("j (p t) -> (j p) t", t=SPREAD), few_rec[:]).then_inc(rec_out, 16)
                sp.wait_ge(rec_out, (n + 1) * 16)
                sp.dma_start(o_rec[:], S["rec"].rearrange("j (a t) -> j a t", a=1).broadcast_to((GRP, HD, CH))).then_inc(rec_in, 16)

            def maxima_row(g, v, part):
                sp.wait_ge(negmax_ready, g * PARTS + part + 1)
                chunks = CHUNKS_OF[part]
                sp.dma_start(qs[v][ONES_ROW:ONES_ROW + 1, chunks[0]:chunks[-1] + 1].bitcast(F32)
                             .rearrange("a c j (b t) -> a (c j b) t", t=P), neg_max[part][:].bitcast(F32)).then_inc(negmax_in[v], 16)

            def one(h, u, weigh, maxima):
                s = h * 2 + u
                gh, v = after(h, u, weigh)
                g = gh * 2 + v
                if weigh and (not isinstance(s, int) or s > 0):
                    reciprocals(s - 1, NCH - 1)
                if not maxima:
                    sp.wait_ge(step_done, s * NS)
                    sp.dma_start(M["wo_raw"][:], io["wo"].rearrange("(k p) n -> p k n", p=P)).then_inc(M["wo_in"], 16)
                if maxima:
                    wait_past(sp, step_done, s * NS)
                    if weigh:
                        load_stacks(sp, "qk", g, v, 0, NCH, load_in[v])
                    else:
                        load_stacks(sp, "q", g, v, 0, 1, first_in[0])
                        for c in range(1, NCH):
                            load_stacks(sp, "q", g, v, c, c + 1, first_in[1])
                if weigh:
                    if not isinstance(s, int) or s > 0:
                        store(s - 1, NCH - 1)
                    reciprocals(s, 0)
                    maxima_row(s, u, 1)
                    store(s, 0)
                    reciprocals(s, 1)
                    maxima_row(s, u, 2)
                    store(s, 1)
                    reciprocals(s, 2)
                    store(s, 2)
                if maxima:
                    maxima_row(g, v, 0)

            passes(sp, one)
            reciprocals(KVH - 1, NCH - 1)
            store(KVH - 1, NCH - 1)
            sp.wait_ge(o_out, KVH * NCH * 32)

        @block.scalar
        def _(act):
            def one(h, u, weigh, maxima):
                s = h * 2 + u

                def copy_out(c):
                    act.wait_ge(step_done, s * NS + LAST[c] + 1)
                    wait_past(act, o_ready, s * NCH + c - 1)
                    nc.scalar.activation(o_sum[:, c % 2], sum_ps, ACT.Copy)
                    nc.scalar.activation(o_raw[:, c % 2], out_ps, ACT.Copy).then_inc(raw_ready, 1)

                if not weigh:
                    wmod_v = io["wmod"].rearrange("(p kk) n -> p kk n", kk=KT)

                    def load(i):
                        n = PIECES[i]
                        act.dma_start(piece[:, i % MOD_RING], wmod_v[:, :, n * MODC:(n + 1) * MODC]).then_inc(piece_in[i % MOD_RING], 16)

                    load_stacks(act, "k", 0, 0, 0, 1, first_in[0])
                    load_stacks(act, "k", 0, 0, 1, NCH, first_in[1])
                    act.wait_ge(first_in[1], REST_LOADS * 16)
                    for i in range(MOD_RING):
                        load(i)
                    for i in range(len(PIECES)):
                        act.wait_ge(piece_used, i + 1)
                        wait_past(act, rows_turned, i - 1)
                        nc.scalar.activation(mod_rows[:, i % 2], rows_ps[:, i % 2], ACT.Copy).then_inc(rows_copied, 1)
                        if i + MOD_RING < len(PIECES):
                            load(i + MOD_RING)
                    act.wait_ge(gate_turned, 2)
                    act.dma_start(S["gates"].rearrange("g (k p) -> (g k) p", p=P), gate_row[:]).then_inc(gate_out, 16)
                    act.wait_ge(gate_out, 16)
                    return
                for n in range(NS):
                    wait_past(act, step_done, s * NS + n - NP + 1)
                    old = (n - NP) % NS
                    oc, okb = STEPS[old]
                    old_last = not maxima and n >= NP
                    if okb in added_up(old_last)[0][oc]:
                        group = s if n >= NP else s - 1
                        if not isinstance(group, int) or group >= 0:
                            act.wait_ge(sum_added, group * NADD + add_after(old_last, oc, okb))
                    for k, ((j0, j1), (c0, c1), _) in enumerate(UNITS_OF[n]):
                        unit = BEFORE[n] + k
                        act.wait_ge(score_ready, s * NU + unit + 1)
                        nc.scalar.activation(probs[:, n % NP, j0:j1, c0:c1], unit_view(unit, j1 - j0, c1 - c0, not maxima), ACT.Exp,
                                             scale=SCORE_SCALE).then_inc(prob_ready, 1)
                        if k == min(1, len(UNITS_OF[n]) - 1) and n - LAG in LAST:
                            copy_out(STEPS[n - LAG][0])
                copy_out(NCH - 1)

            passes(act, one)
            act.wait_ge(M["wo_in"], 16)
            act.wait_ge(step_done, KVH * NS)
            for kt in range(KT):
                nc.scalar.activation(M["wo_hi"][:, kt], M["wo_raw"][:, kt], ACT.Copy).then_inc(wo_hi_ready, 1)

        @block.gpsimd
        def _(pool):
            nc.gpsimd.memset(ones[:], 1.0).then_inc(ones_ready, 1)
            nc.gpsimd.memset(q_max[:], 0.0).then_inc(ones_ready, 1)
            for c in range(NCH):
                nc.gpsimd.memset(part_max[:, c * TPC, c + 1], MASKED).then_inc(ones_ready, 1)
            for v in range(2):
                pool.wait_ge(ones_ready, v + 2 + NCH)
                nc.gpsimd.memset(ks[v][ONES_ROW:ONES_ROW + 1].bitcast(F32), 1.0).then_inc(ones_ready, 1)

            def one(h, u, weigh, maxima):
                s = h * 2 + u
                if not weigh:
                    return
                def split(c, s):
                    pool.wait_ge(hi_ready, s * NCH + c + 1)
                    wait_past(pool, o_out, (s * NCH + c) * 32)
                    nc.gpsimd.tensor_tensor(o_lo[:], o_full[:], o_hi[:].bitcast(F32), ALU.subtract).then_inc(split_ready, 1)

                if not isinstance(s, int) or s > 0:
                    split(NCH - 1, s - 1)
                ADDED, ADDS = added_up(not maxima)
                for c in range(1, NCH):
                    total = sums[:, (c - 1) % 2]
                    for i, kb in enumerate(ADDED[c][1:]):
                        n = STEPS.index((c, kb))
                        if i == 0 and c != NCH - 1:
                            wait_past(pool, step_done, (s - 1) * NS + LAST[NCH - 1] + 1 if c == 1 else 0)
                        elif i == 0:
                            pool.wait_ge(step_done, s * NS + LAST[1] + 1)
                        pool.wait_ge(prob_ready, s * NU + BEFORE[n + 1])
                        if i:
                            pool.wait_ge(sum_added, s * NADD + sum(ADDS[:c]) + i)
                        first = probs[:, STEPS.index((c, ADDED[c][0])) % NP] if i == 0 else total
                        nc.gpsimd.tensor_tensor(total, first, probs[:, n % NP], ALU.add).then_inc(sum_added, 1)
                        if i == min(4, ADDS[c] - 1):
                            split(c - 1, s)

            passes(pool, one)
            pool.wait_ge(hi_ready, KVH * NCH)
            pool.wait_ge(o_out, (KVH * NCH - 1) * 32)
            nc.gpsimd.tensor_tensor(o_lo[:], o_full[:], o_hi[:].bitcast(F32), ALU.subtract).then_inc(split_ready, 1)

        @block.vector
        def _(dve):
            dve.wait_ge(ones_ready, 4 + NCH)

            def modulation():
                cols, mod, done = score_ps[:, 0], M["mod"], 0

                def link(ins):
                    nonlocal done
                    done += 1
                    ins.then_inc(mod_chain, 1)
                    dve.wait_ge(mod_chain, done)

                dve.wait_ge(rows_turned, len(PIECES))
                nc.vector.tensor_copy(mod[:, 2, :], cols[:, SB_AT:SB_AT + KT])
                nc.vector.tensor_scalar_add(mod[:, 3, :], cols[:, CB_AT:CB_AT + KT], 1.0)
                nc.vector.tensor_copy(gate_col[:, 0], cols[:, GA_AT:GA_AT + KT])
                link(nc.vector.tensor_copy(gate_col[:, 1], cols[:, GB_AT:GB_AT + KT]))
                link(nc.vector.tensor_scalar(gate_neg[:], gate_col[:], -1.0, None, ALU.mult))
                link(nc.vector.tensor_tensor(gate_abs[:], gate_col[:], gate_neg[:], ALU.max))
                link(nc.vector.tensor_scalar(gate_sgn[:], gate_col[:], 0.0, 2.0, ALU.is_ge, ALU.mult))
                link(nc.vector.tensor_scalar(gate_neg[:], gate_sgn[:], 1.0, None, ALU.subtract))
                link(nc.vector.tensor_scalar(gate_sgn[:], gate_abs[:], 0.25, None, ALU.max))
                nc.vector.tensor_tensor(gate_fin[:], gate_sgn[:], gate_neg[:], ALU.mult).then_inc(gate_ready, 1)
                dve.wait_ge(gate_turned, 1)
                nc.vector.tensor_copy(gate_row[:], score_ps[0:2 * KT, 1, 0:P]).then_inc(gate_turned, 1)

            def reciprocals(s, c):
                n = s * NCH + c
                dve.wait_ge(sum_in, (n + 1) * GRP * 16)
                nc.vector.reciprocal(few_rec[:], few_sum[:]).then_inc(rec_ready, 1)

            def normalise(s, c):
                n = s * NCH + c
                dve.wait_ge(rec_in, (n + 1) * 16)
                wait_past(dve, split_ready, n)
                wait_past(dve, o_out, n * 32)
                nc.vector.tensor_tensor(o_full[:], o_raw[:, c % 2], o_rec[:], ALU.mult).then_inc(o_ready, 1)
                dve.wait_ge(o_ready, n + 1)
                nc.vector.tensor_copy(o_hi[:], o_full[:]).then_inc(hi_ready, 1)

            def one(h, u, weigh, maxima):
                s = h * 2 + u
                gh, v = after(h, u, weigh)
                g = gh * 2 + v
                own, following = schedule(weigh, maxima)

                def values_of_group():
                    wait_past(dve, step_done, s * NS)
                    nc.vector.tensor_copy(v_g[v][:], v_all[:, :, bass.ds(g * HD, HD)]).then_inc(v_ready, 1)

                def negate(g, gh, v, part):
                    dve.wait_ge(maxt_ready, g * PARTS + part + 1)
                    if not isinstance(g, int) or g > 0:
                        dve.wait_ge(negmax_in[1 - v], (gh + v - 1) * PARTS * 16 + 16 * (part + 1))
                    rows = neg_max[part].shape[0]
                    nc.vector.tensor_scalar(neg_max[part][:], max_ps[0:rows, 0, 0, 0:P], -1.0, None,
                                            ALU.mult).then_inc(negmax_ready, 1)

                def take_max(g, gh, v, m):
                    if m in TURN:
                        negate(g, gh, v, TURN.index(m))
                        return
                    dve.wait_ge(max_ready, g * NM + m + 1)
                    qb, slot, _, _, (kind, hp, w) = MAXES[m]
                    banks = max_ps[:, m % 2]
                    if kind == "pair":
                        src, dst = banks[:, :, 0:w], part_max[:, qb, slot, 2 * hp:2 * hp + 2]
                    elif kind == "four":
                        src, dst = banks.rearrange("p b (j t) -> p (b j) t", t=w), part_max[:, qb, slot]
                    elif kind == "diag":
                        src, dst = banks[:, 0].rearrange("p (j t) -> p j t", t=w), part_max[:, qb, slot]
                    else:
                        src = banks.rearrange("p b (j t) -> p (b j) t", t=w)
                        dst = part_max[:, qb, slot:slot + 2].rearrange("p e j -> p (e j)")
                    nc.vector.tensor_reduce(dst, src, op=ALU.max, axis=AX.X).then_inc(max_read, 1)
                    if m + 1 in END_OF_PART:
                        part = END_OF_PART.index(m + 1)
                        dve.wait_ge(max_read, g * NM + m + 1)
                        for i, c in enumerate(CHUNKS_OF[part]):
                            tiles = slice(c * TPC, (c + 1) * TPC)
                            place = q_max[:, part, i * GRP * TPC:(i + 1) * GRP * TPC]
                            last = nc.vector.tensor_reduce(place.rearrange("p (j b) -> p b j", j=GRP),
                                                           part_max[:, tiles, 0:c + 2].rearrange("p b e j -> p b j e"),
                                                           op=ALU.max, axis=AX.X)
                        last.then_inc(qmax_ready, 1)

                if not weigh:
                    values_of_group()
                    for m in following[0]:
                        take_max(g, gh, v, m)
                    modulation()
                    return
                for n in range(NS):
                    if n == COPY_V and maxima:
                        values_of_group()
                    for m in own[n]:
                        take_max(s, h, u, m)
                    for m in following[n]:
                        take_max(g, gh, v, m)
                    for lag, work in ((REC_LAG, reciprocals), (NORM_LAG, normalise)):
                        if n - lag in LAST:
                            work(s, STEPS[n - lag][0])
                        if n - lag + NS in LAST and (not isinstance(s, int) or s > 0):
                            work(s - 1, STEPS[n - lag + NS][0])

            passes(dve, one)
            for kt in range(KT):
                if kt == 2:
                    reciprocals(KVH - 1, NCH - 1)
                if kt == 6:
                    normalise(KVH - 1, NCH - 1)
                dve.wait_ge(wo_hi_ready, kt + 1)
                nc.vector.tensor_tensor(M["wo_lo"][:, kt], M["wo_raw"][:, kt], M["wo_hi"][:, kt].bitcast(F32), ALU.subtract)

        @block.tensor
        def _(pe):
            pe.wait_ge(ones_ready, 4 + NCH)

            def one(h, u, weigh, maxima):
                s = h * 2 + u
                gh, v = after(h, u, weigh)
                g = gh * 2 + v
                own, following = schedule(weigh, maxima)

                def max_unit(g, gh, v, m):
                    if m in TURN:
                        part = TURN.index(m)
                        pe.wait_ge(qmax_ready, g * PARTS + part + 1)
                        nc.tensor.transpose(max_ps[:, 0, 0, 0:P], q_max[:, part], ident[:]).then_inc(maxt_ready, 1)
                        return
                    if not weigh and m in FIRST_OF_CHUNK[:2]:
                        pe.wait_ge(first_in[FIRST_OF_CHUNK.index(m)], (REST_LOADS if m else LOADS) * 16)
                    if m == 0 and weigh:
                        pe.wait_ge(load_in[v], (gh + v) * LOADS * 16)
                        wait_past(pe, negmax_ready, g * PARTS)
                    for part in range(PARTS - 1):
                        if m == END_OF_PART[part] + END_OF_PART[part] % 2:
                            pe.wait_ge(negmax_ready, g * PARTS + part + 1)
                    if m >= 2:
                        pe.wait_ge(max_read, g * NM + m - 1)
                    qb, _, pieces, diag, _ = MAXES[m]
                    for i, (b, at, j, k0, kn) in enumerate(pieces):
                        first = i == 0 or pieces[i - 1][0] != b
                        final = i == len(pieces) - 1 or pieces[i + 1][0] != b
                        last = nc.tensor.matmul(max_ps[:, m % 2, b, at:at + kn], qs[v][0:ONES_ROW, qb // TPC, j, qb % TPC * P:(qb % TPC + 1) * P],
                                                ks[v][0:ONES_ROW, k0:k0 + kn], start=first, stop=final and diag != b)
                        if final and diag == b:
                            last = nc.tensor.matmul(max_ps[:, m % 2, b].rearrange("p (j t) -> p j t", t=P), ident_b,
                                                    four(mask_qk), start=False, stop=True)
                    last.then_inc(max_ready, 1)

                if not weigh:
                    done = 0

                    def turn(i):
                        pe.wait_ge(rows_copied, i + 1)
                        turn_piece(nc, score_ps[:, 0], mod_rows[:, i % 2], M["pick"], i * (MODC // P)).then_inc(rows_turned, 1)

                    for i, m in enumerate(following[0]):
                        max_unit(g, gh, v, m)
                        while done < len(PIECES) and (i - FIRST_PIECE + 1) * len(PIECES) >= (done + 1) * (EARLY - 1 - FIRST_PIECE):
                            pe.wait_ge(piece_in[done % MOD_RING], 16 * (done // MOD_RING + 1))
                            wait_past(pe, rows_copied, done - 1)
                            multiply_piece(nc, rows_ps[:, done % 2], piece[:, done % MOD_RING], M["c_act"]).then_inc(piece_used, 1)
                            if done:
                                turn(done - 1)
                            done += 1
                    assert done == len(PIECES)
                    turn(len(PIECES) - 1)
                    pe.wait_ge(gate_ready, 1)
                    nc.tensor.transpose(score_ps[0:2 * KT, 1, 0:P], gate_fin[:].rearrange("p g k -> p (g k)"),
                                        ident[:]).then_inc(gate_turned, 1)
                    pe.wait_ge(gate_turned, 2)
                    return

                def scores(n, part):
                    c, kb = STEPS[n]
                    if kb == 0 and part == 0:
                        for p in range(1, PARTS):
                            if c == CHUNKS_OF[p][0]:
                                pe.wait_ge(negmax_in[u], h * PARTS * 16 + (p + 1) * 16)
                    for k, ((j0, j1), (c0, c1), masked) in enumerate(UNITS_OF[n]):
                        if (k >= 2) != (part == 1):
                            continue
                        unit = BEFORE[n] + k
                        wide = unit - WIDE_FROM
                        if maxima or wide < 2:
                            wait_past(pe, prob_ready, s * NU + unit - 1)
                        elif wide >= len(WIDE_BANKS):
                            pe.wait_ge(prob_ready, s * NU + unit + 1 - len(WIDE_BANKS))
                        out = unit_view(unit, j1 - j0, c1 - c0, not maxima)
                        last = nc.tensor.matmul(out, ks[u][:, kb * P:(kb + 1) * P], qs[u][:, c, j0:j1, c0:c1],
                                                start=True, stop=not masked)
                        if masked:
                            last = nc.tensor.matmul(out, ident_b, four(mask_kq), start=False, stop=True)
                        last.then_inc(score_ready, 1)

                def values(n):
                    c, kb = STEPS[n]
                    off = max(0, kb * P - c * CH)
                    if kb == 0:
                        wait_past(pe, raw_ready, s * NCH + c)
                    pe.wait_ge(prob_ready, s * NU + BEFORE[n + 1])
                    for j in range(GRP):
                        last = nc.tensor.matmul(out_ps[j * HD:(j + 1) * HD, off:], v_g[u][:, kb], probs[:, n % NP, j, off:],
                                                start=(kb == 0), stop=n in LAST)
                    if not sums_of(n):
                        last.then_inc(step_done, 1)

                ADDED, ADDS = added_up(not maxima)

                def sums_of(n):
                    c, kb = STEPS[n]
                    own = [] if kb in ADDED[c] else [(probs[:, n % NP], max(0, kb * P - c * CH))]
                    return own + ([(sums[:, (c - 1) % 2], 0)] if n in LAST and ADDED[c] else [])

                def row_sums(n):
                    c, kb = STEPS[n]
                    summed = sums_of(n)
                    begin = kb == min(b for b in range(NTT) if b not in ADDED[c])
                    for i, (tile, at) in enumerate(summed):
                        if i == 1:
                            pe.wait_ge(sum_added, s * NADD + sum(ADDS[:c + 1]))
                        for j in range(GRP):
                            last = nc.tensor.matmul(sum_ps[j * HD:(j + 1) * HD, at:], ones[:], tile[:, j, at:], start=begin,
                                                    stop=n in LAST and i == len(summed) - 1)
                    if summed:
                        last.then_inc(step_done, 1)

                pe.wait_ge(v_ready, s + 1)
                pe.wait_ge(negmax_in[u], h * PARTS * 16 + 16)
                for n in range(NS + LAG):
                    units = [(s, h, u, m) for m in own[n]] + [(g, gh, v, m) for m in following[n]] if n < NS else []
                    late = n < NS and n >= LAG and n - LAG not in LAST and sums_of(n - LAG)
                    places = (PLACES_SUMS if late else PLACES)[min(4, len(units))]

                    def maxima_at(place):
                        for k, unit in enumerate(units):
                            if places[min(k, 3)] == place:
                                max_unit(*unit)

                    if n < NS:
                        scores(n, 0)
                    maxima_at(0)
                    if n >= LAG:
                        values(n - LAG)
                        if not late:
                            row_sums(n - LAG)
                    maxima_at(1)
                    if n < NS:
                        scores(n, 1)
                    maxima_at(2)
                    if late:
                        row_sums(n - LAG)
                    maxima_at(3)

            passes(pe, one)


def feed_block(nc, io, S, M):
    ctx = ExitStack()
    with ctx:
        def sb(name, shape, dt=F32):
            return ctx.enter_context(nc.sbuf_tensor(name, shape, dt))

        def sem(name):
            return ctx.enter_context(nc.semaphore(name))

        RING = 4
        wo_hi, wo_lo = M["wo_hi"], M["wo_lo"]
        down = sb("router_and_a", [P, KT, EXPERTS + ER])
        up = sb("lora_b", [P, D])
        gates = sb("gates", [P, 2, D])
        o_hi = sb("att_hi", [P, 2, KVH, P], F32R)
        o_lo = sb("att_lo", [P, 2, KVH, P], F32R)
        x_t = sb("x_tile", [P, 2, D])
        gated = sb("gated", [P, D])
        x1 = sb("x_mid", [P, RING, D])
        xn = sb("x_mid_normed", [P, D])
        h_t = sb("h_transposed", [P, KT, P])
        cell = sb("hold_cell2", [P, 1])
        top = sb("top_logit", [P, 1])
        top_rank = sb("top_rank", [P, 1])
        rank = sb("rank_where_top", [P, EXPERTS])
        route = sb("route_weight", [P, EXPERTS])
        wh = sb("weighted_h", [P, ER])
        wh_t = sb("weighted_h_t", [P, P])
        lora = sb("lora_gated", [P, D])
        y = sb("y_tile", [P, 2, D])
        stats = sb("ln2_stats", [P, 2, 6])
        meanvar = sb("ln2_meanvar", [P, 2])
        var = sb("ln2_var", [P, 1])
        std = sb("ln2_std", [P, 1])
        r0 = sb("ln2_r0", [P, 1])
        r1 = sb("ln2_r1", [P, 1])
        r2 = sb("ln2_r2", [P, 1])
        rstd = sb("ln2_rstd", [P, 1])
        ident, mod, ranks = M["ident"], M["mod"], M["ranks"]
        proj_ps = M["psum"][:, 0:2]
        tr_ps = M["psum"][:, 2:4].rearrange("p b (k t) -> p (b k) t", t=P)
        down_ps = M["psum"][:, 4]
        wht_ps = M["psum"][:, 5, 0:P]
        up_ps = M["psum"][:, 6:8]

        small_in = sem("small_in")
        o_in = [sem(f"att_in{i}") for i in range(2)]
        x_in = [sem(f"x_tile_in{i}") for i in range(2)]
        y_out = [sem(f"y_out{i}") for i in range(2)]
        proj_ready = sem("proj_ready")
        proj_read = sem("proj_read")
        x1_ready = sem("x1_ready")
        var_ready = sem("var2_ready")
        std_ready = sem("std2_ready")
        xn_ready = sem("xn2_ready")
        tr_ready = sem("tr2_ready")
        h_ready = sem("h2_ready")
        down_ready = sem("down_ready")
        wh_ready = sem("wh_ready")
        wht_ready = sem("wht_ready")
        wht_read = sem("wht_read")
        up_ready = sem("up_ready")
        up_read = sem("up_read")
        y_ready = sem("y_ready")
        chain0, chain1 = sem("norm_chain"), sem("route_chain")
        block = ctx.enter_context(nc.Block())

        def steps(eng, step):
            for t in range(RING):
                step(t, t, t // 2, True, t >= 1, t >= 2)
            with eng.Fori(1, NTT // RING) as i:
                for r in range(RING):
                    step(i * RING + r, r, i * (RING // 2) + r // 2, True, True, True)
            step(NTT, 0, NTT // 2, False, True, True)
            step(NTT + 1, 1, NTT // 2, False, False, True)

        @block.sync
        def _(sp):
            def step(t, r, pairs, has0, has1, has2):
                if has0:
                    wait_past(sp, proj_ready, (t - 1) * 2)
                    for part, tile in ((0, o_hi), (1, o_lo)):
                        sp.dma_start(tile[:, r % 2].bitcast(F32), S["o"][part, :, :, bass.ds(t * P, P)].rearrange("g p t -> p g t"))\
                          .then_inc(o_in[r % 2], 16)
                    wait_past(sp, x1_ready, (t - 1) * 2)
                    sp.dma_start(x_t[:, r % 2], io["x"][bass.ds(t * P, P), :]).then_inc(x_in[r % 2], 16)
                if has2:
                    sp.wait_ge(y_ready, t - 1)
                    sp.dma_start(io["out"][bass.ds((t - 2) * P, P), :], y[:, r % 2]).then_inc(y_out[r % 2], 16)

            steps(sp, step)
            for i in range(2):
                sp.wait_ge(y_out[i], NTT // 2 * 16)

        @block.scalar
        def _(act):
            act.dma_start(gates[:], S["gates"].partition_broadcast(P)).then_inc(small_in, 16)
            act.dma_start(down[:], io["down"].rearrange("(k p) n -> p k n", p=P)).then_inc(small_in, 16)
            act.dma_start(up[:], io["up"]).then_inc(small_in, 16)

            def step(t, r, pairs, has0, has1, has2):
                if has2:
                    act.wait_ge(wht_ready, t - 1)
                    wait_past(act, up_ready, t - 2)
                    nc.scalar.activation(wh_t[:], wht_ps, ACT.Copy).then_inc(wht_read, 1)
                if has1:
                    act.wait_ge(tr_ready, t)
                    wait_past(act, down_ready, t - 1)
                    for kt in range(KT):
                        last = nc.scalar.activation(h_t[:, kt], tr_ps[:, kt], ACT.Identity, bias=mod[:, 2, kt:kt + 1],
                                                    scale=mod[:, 3, kt:kt + 1])
                    last.then_inc(h_ready, 1)
                if has0:
                    act.wait_ge(var_ready, t + 1)
                    nc.scalar.activation(std[:], var[:], ACT.Sqrt).then_inc(std_ready, 1)

            steps(act, step)

        @block.vector
        def _(dve):
            dve.wait_ge(small_in, 48)
            NORM_LINKS, ROUTE_LINKS = 9, 4

            class Chain:

                def __init__(self, which, base):
                    self.which, self.base, self.k = which, base, 0

                def link(self, ins):
                    self.k += 1
                    ins.then_inc(self.which, 1)

                def wait(self):
                    dve.wait_ge(self.which, self.base + self.k)

            def residual(t, r, pairs, half, norm):
                cols = slice(half * CH, (half + 1) * CH)
                dve.wait_ge(proj_ready, t * 2 + half + 1)
                if half == 0:
                    dve.wait_ge(x_in[r % 2], (pairs + 1) * 16)
                nc.vector.tensor_tensor(gated[:, cols], proj_ps[:, half], gates[:, 0, cols], ALU.mult).then_inc(proj_read, 1)
                dve.wait_ge(proj_read, t * 2 + half + 1)
                nc.vector.tensor_tensor(x1[:, r, cols], gated[:, cols], x_t[:, r % 2, cols], ALU.add).then_inc(x1_ready, 1)
                dve.wait_ge(x1_ready, t * 2 + half + 1)
                norm.link(nc.vector.bn_stats(stats[:, half], x1[:, r, cols]))

            def finish_norm(t, r, norm):
                norm.wait()
                norm.link(nc.vector.tensor_copy(cell[:], ident[:, 0:1]))
                norm.link(nc.vector.bn_aggr(meanvar[:], stats[:]))
                norm.wait()
                nc.vector.tensor_scalar_add(var[:], meanvar[:, 1:2], LN_EPS).then_inc(var_ready, 1)
                dve.wait_ge(std_ready, t + 1)
                norm.link(nc.vector.reciprocal(r0[:], std[:]))
                norm.wait()
                norm.link(nc.vector.tensor_tensor(r1[:], r0[:], r0[:], ALU.mult))
                norm.wait()
                norm.link(nc.vector.tensor_tensor(r2[:], r1[:], var[:], ALU.mult))
                norm.wait()
                norm.link(nc.vector.tensor_scalar(r1[:], r2[:], -0.5, 1.5, ALU.mult, ALU.add))
                norm.wait()
                norm.link(nc.vector.tensor_tensor(rstd[:], r0[:], r1[:], ALU.mult))
                norm.wait()
                assert norm.k == NORM_LINKS
                wait_past(dve, tr_ready, t)
                nc.vector.tensor_scalar(xn[:], x1[:, r], meanvar[:, 0:1], rstd[:], ALU.subtract, ALU.mult).then_inc(xn_ready, 1)

            def route_tile(t):
                c = Chain(chain1, t * ROUTE_LINKS)
                dve.wait_ge(down_ready, t + 1)
                logits = down_ps[:, 0:EXPERTS]
                c.link(nc.vector.tensor_reduce(top[:], logits, op=ALU.max, axis=AX.X))
                c.wait()
                c.link(nc.vector.scalar_tensor_tensor(out=rank[:], in0=logits, scalar=top[:], in1=ranks[:],
                                                      op0=ALU.is_equal, op1=ALU.mult))
                c.wait()
                c.link(nc.vector.tensor_reduce(top_rank[:], rank[:], op=ALU.max, axis=AX.X))
                c.wait()
                c.link(nc.vector.tensor_scalar(route[:], rank[:], top_rank[:], top[:], ALU.is_equal, ALU.mult))
                c.wait()
                assert c.k == ROUTE_LINKS
                wait_past(dve, wht_ready, t)
                nc.vector.tensor_tensor(wh[:].rearrange("p (e r) -> p e r", r=RANK),
                                        down_ps[:, EXPERTS:EXPERTS + ER].rearrange("p (e r) -> p e r", r=RANK),
                                        route[:].rearrange("p (e a) -> p e a", a=1).broadcast_to((P, EXPERTS, RANK)),
                                        ALU.mult).then_inc(wh_ready, 1)

            def output(t, r, pairs):
                dve.wait_ge(up_ready, t + 1)
                nc.vector.tensor_tensor(lora[:].rearrange("p (b n) -> p b n", b=2), up_ps,
                                        gates[:, 1].rearrange("p (b n) -> p b n", b=2), ALU.mult).then_inc(up_read, 1)
                dve.wait_ge(up_read, t + 1)
                wait_past(dve, y_out[r % 2], pairs * 16)
                nc.vector.tensor_tensor(y[:, r % 2], lora[:], x1[:, r], ALU.add).then_inc(y_ready, 1)

            def step(t, r, pairs, has0, has1, has2):
                norm = Chain(chain0, t * NORM_LINKS)
                if has0:
                    residual(t, r, pairs, 0, norm)
                if has2:
                    output(t - 2, (r - 2) % RING, pairs - 1)
                if has0:
                    residual(t, r, pairs, 1, norm)
                if has1:
                    route_tile(t - 1)
                if has0:
                    finish_norm(t, r, norm)

            steps(dve, step)

        @block.tensor
        def _(pe):
            def project(t, r, pairs, half):
                cols = slice(half * CH, (half + 1) * CH)
                if half == 0:
                    pe.wait_ge(o_in[r % 2], (pairs + 1) * 32)
                wait_past(pe, proj_read, (t - 1) * 2 + half + 1)
                for g in range(KVH):
                    terms = ((o_hi[:, r % 2, g], wo_hi[:, g, cols]), (o_hi[:, r % 2, g], wo_lo[:, g, cols]),
                             (o_lo[:, r % 2, g], wo_hi[:, g, cols]))
                    for i, (lhs, rhs) in enumerate(terms):
                        last = nc.tensor.matmul(proj_ps[:, half], lhs, rhs, start=g == 0 and i == 0, stop=g == KVH - 1 and i == 2)
                last.then_inc(proj_ready, 1)

            def step(t, r, pairs, has0, has1, has2):
                if has0:
                    project(t, r, pairs, 0)
                if has2:
                    pe.wait_ge(wh_ready, t - 1)
                    wait_past(pe, wht_read, t - 2)
                    nc.tensor.transpose(wht_ps, wh[:], ident[:]).then_inc(wht_ready, 1)
                if has1:
                    pe.wait_ge(xn_ready, t)
                    wait_past(pe, h_ready, t - 1)
                    for kt in range(KT):
                        last = nc.tensor.transpose(tr_ps[:, kt], xn[:, kt * P:(kt + 1) * P], ident[:])
                    last.then_inc(tr_ready, 1)
                if has2:
                    if isinstance(t, int) and t == 2:
                        pe.wait_ge(small_in, 48)
                    pe.wait_ge(wht_read, t - 1)
                    wait_past(pe, up_read, t - 2)
                    for b in range(2):
                        last = nc.tensor.matmul(up_ps[:, b], wh_t[:], up[:, b * CH:(b + 1) * CH], start=True, stop=True)
                    last.then_inc(up_ready, 1)
                if has0:
                    project(t, r, pairs, 1)
                if has1:
                    if isinstance(t, int) and t == 1:
                        pe.wait_ge(small_in, 48)
                    pe.wait_ge(h_ready, t)
                    wait_past(pe, wh_ready, t - 1)
                    for kt in range(KT):
                        last = nc.tensor.matmul(down_ps[:, 0:EXPERTS + ER], h_t[:, kt], down[:, kt], start=kt == 0, stop=kt == KT - 1)
                    last.then_inc(down_ready, 1)

            steps(pe, step)


def build_program(nc, io, out):
    io = dict(io, out=out)
    S = {
        "gates": nc.dram_tensor("gate_rows", [2, D], F32, kind="Internal").ap(),
        "q": nc.dram_tensor("q_split", [2, 2, HEADS, HALF, T], F32, kind="Internal").ap(),
        "k": nc.dram_tensor("k_split", [2, 2, KVH, HALF, T], F32, kind="Internal").ap(),
        "rec": nc.dram_tensor("reciprocals", [GRP, CH], F32, kind="Internal").ap(),
        "o": nc.dram_tensor("attention_split", [2, KVH, P, T], F32, kind="Internal").ap(),
    }
    ctx = ExitStack()
    with ctx:
        def sb(name, shape, dt=F32):
            return ctx.enter_context(nc.sbuf_tensor(name, shape, dt))

        M = {
            "ident": sb("identity", [P, P]),
            "ranks": sb("expert_ranks", [P, EXPERTS]),
            "masks": sb("masks_bf16", [P, 3, P], BF16),
            "mod": sb("modulation", [P, 4, KT]),
            "c_act": sb("silu_c", [P, KT, HD]),
            "pick": sb("pick_row", [P, 1]),
            "psum": ctx.enter_context(nc.psum_tensor("psum_banks", [P, 8, CH], F32)),
        }
        with ExitStack() as upto_feed:
            M["v_all"] = upto_feed.enter_context(nc.sbuf_tensor("v_all", [P, NTT, KV_W], F32))
            with ExitStack() as upto_project:
                M["w_hi"] = upto_project.enter_context(nc.sbuf_tensor("w_hi", [P, KT, WCOLS], F32R))
                M["w_lo"] = upto_project.enter_context(nc.sbuf_tensor("w_lo", [P, KT, WCOLS], F32R))
                M["x"] = upto_project.enter_context(nc.sbuf_tensor("x_chunk", [P, TPC, D], F32))
                M["x_in"] = [upto_project.enter_context(nc.semaphore(f"x_in{j}")) for j in range(TPC)]
                modulate_block(nc, io, S, M)
                project_block(nc, io, S, M)
            with ExitStack() as place:
                M["q_stack0"] = place.enter_context(nc.sbuf_tensor("q_stack0", [3 * HD + 1, NCH, GRP, CH], F32R))
            M["wo_raw"] = upto_feed.enter_context(nc.sbuf_tensor("wo_raw", [P, KT, D], F32))
            M["wo_in"] = upto_feed.enter_context(nc.semaphore("wo_in"))
            with ExitStack() as place:
                M["wmod_piece2"] = place.enter_context(nc.sbuf_tensor("wmod_piece2", [P, MOD_RING, KT, MODC], F32))
            with ExitStack() as place:
                M["probs"] = place.enter_context(nc.sbuf_tensor("probs", [P, NP, GRP, CH], F32))
            M["wo_hi"] = upto_feed.enter_context(nc.sbuf_tensor("wo_hi", [P, KT, D], F32R))
            M["wo_lo"] = upto_feed.enter_context(nc.sbuf_tensor("wo_lo", [P, KT, D], F32R))
            attend_block(nc, io, S, M)
            feed_block(nc, io, S, M)


def shape_constants():
    base = np.float32(500000.0)
    exponent = np.arange(0, HD, 2, dtype=np.float32) / np.float32(HD)
    inv_freq = np.float32(1.0) / np.power(np.float64(base), exponent.astype(np.float64)).astype(np.float32)
    angle = np.arange(T, dtype=np.float32)[None, :] * inv_freq[:, None]
    trig = np.stack([np.cos(angle), np.sin(angle)], axis=1).astype(np.float32)
    trig = np.ascontiguousarray(np.tile(trig, (P // HALF, 1, 1)))
    consts = np.zeros((P, P + EXPERTS), np.float32)
    consts[:, :P] = np.eye(P)
    consts[:, P:] = EXPERTS - np.arange(EXPERTS)
    row, col = np.arange(P)[:, None], np.arange(P)[None, :]
    masks = np.stack([np.eye(P), np.where(col > row, MASKED, 0.0), np.where(row > col, MASKED, 0.0)], axis=1)
    return trig, consts, masks.astype(mybir.dt.np(BF16))


def kernel(**inputs):
    import concourse.bacc as bacc
    from concourse.bass_utils import run_bass_kernel_spmd

    a = {k: np.asarray(v) for k, v in inputs.items()}
    trig, consts, masks = shape_constants()
    wq = a["L0_attn_Wq"].reshape(D, QUNITS, HPU, 2, HALF).transpose(0, 1, 3, 2, 4).reshape(D, HEADS * HD)
    wk = a["L0_attn_Wk"].reshape(D, KVH, 2, HALF).transpose(0, 2, 1, 3).reshape(D, KV_W)
    arrays = {
        "x": a["L0_attn_x"].reshape(T, D),
        "wqkv": np.concatenate([wk, a["L0_attn_Wv"], wq], axis=1),
        "wo": a["L0_attn_Wo"],
        "down": np.concatenate([a["L0_ffn_route_w"], a["L0_ffn_A"].reshape(ER, D)], axis=0).T,
        "up": a["L0_ffn_Bw"].transpose(0, 2, 1).reshape(ER, D),
        "c": a["L0_c"],
        "wmod": a["L0_wmod"],
        "trig": trig,
        "consts": consts,
        "masks": masks,
    }
    nc = bacc.Bacc("TRN2", target_bir_lowering=False, num_devices=1)
    feeds, io = {}, {}
    for name, array in arrays.items():
        array = np.ascontiguousarray(array)
        feeds[f"in_{name}"] = array
        io[name] = nc.dram_tensor(f"in_{name}", array.shape, mybir.dt.from_np(array.dtype), kind="ExternalInput").ap()
    out = nc.dram_tensor("out_x", (T, D), F32, kind="ExternalOutput").ap()
    build_program(nc, io, out)
    result = run_bass_kernel_spmd(nc, [feeds], core_ids=[0])
    return result.results[0]["out_x"].reshape(1, T, D)
```
